# Optimizing a Trainium2 kernel written in Bass

```python
import numpy as np
import jax
import jax.numpy as jnp

def _softmax(x, axis=-1):
    return jax.nn.softmax(x, axis=axis)

def _gelu(x):
    return jax.nn.gelu(x, approximate=True)

def _silu(x):
    return jax.nn.silu(x)

def _sigmoid(x):
    return jax.nn.sigmoid(x)

def _layernorm(x, axis=-1, eps=1e-05):
    m = jnp.mean(x, axis=axis, keepdims=True)
    v = jnp.var(x, axis=axis, keepdims=True)
    return (x - m) / jnp.sqrt(v + eps)

def _scatter_add(tgt, idx, src, axis=0):
    return tgt.at[idx].add(src)

def _segment_sum(src, seg, n):
    return jax.ops.segment_sum(src, seg, n)
kernel_name = 'mk_gnn_resnorm_d2_gnn_r8_ab39b9'

def setup_inputs(seed: int=0):
    np.random.seed(seed)
    _w = jnp.asarray

    def _rec_inputs():
        import jax
        import jax.numpy as jnp
        _gk = jax.random.key(seed)
        x = -0.0002928 + 1 * jax.random.normal(jax.random.fold_in(_gk, 1), (1024, 512), jnp.float32)
        src = jax.random.randint(jax.random.fold_in(_gk, 2), (16384,), 0, 1024, jnp.int32)
        dst = jax.random.randint(jax.random.fold_in(_gk, 3), (16384,), 0, 1024, jnp.int32)
        _o = jnp.argsort(dst, stable=True)
        src = src[_o]
        dst = dst[_o]
        edge_weight = jax.random.uniform(jax.random.fold_in(_gk, 12), (16384,), jnp.float32, 0.0, 0.999994)
        return (x, src, dst, edge_weight)
    x, src, dst, edge_weight = _rec_inputs()

    def _L0_gnn_setup():
        import jax, jax.numpy as jnp
        import numpy as np
        N_NODES = 1024
        D_MODEL = 512
        N_LAYERS = 2
        N_EDGES = 32768
        LEAKY_SLOPE = 0.01

        def _normalized_adj(edge_index, edge_weights, num_nodes):
            A = jnp.zeros((num_nodes, num_nodes), dtype=edge_weights.dtype)
            A = A.at[edge_index[0], edge_index[1]].add(edge_weights)
            deg = jnp.sum(A, axis=1)
            dinv = jnp.where(deg > 0, deg ** (-0.5), 0.0)
            return dinv[:, None] * A * dinv[None, :]
        key = jax.random.key(seed)
        ks = jax.random.split(key, 6)
        x = jax.random.normal(ks[0], (N_NODES, D_MODEL), dtype=jnp.float32)
        edge_weights = jax.random.uniform(ks[1], (N_EDGES,), dtype=jnp.float32)
        edge_index = jax.random.randint(ks[2], (2, N_EDGES), 0, N_NODES, dtype=jnp.int64)
        scale = 0.02
        W_gcn = jax.random.normal(ks[3], (N_LAYERS, D_MODEL, D_MODEL), dtype=jnp.float32) * scale
        b_gcn = jnp.zeros((N_LAYERS, D_MODEL), dtype=jnp.float32)
        W_mlp = jax.random.normal(ks[4], (N_LAYERS, D_MODEL, D_MODEL), dtype=jnp.float32) * scale
        b_mlp = jnp.zeros((N_LAYERS, D_MODEL), dtype=jnp.float32)
        return {'x': x, 'edge_weights': edge_weights, 'W_gcn': W_gcn, 'b_gcn': b_gcn, 'W_mlp': W_mlp, 'b_mlp': b_mlp, 'edge_index': edge_index}
    _L0_gnn_all = _L0_gnn_setup()
    _L0_gnn_in = {k: v for k, v in _L0_gnn_all.items() if k in ('W_gcn', 'b_gcn', 'W_mlp', 'b_mlp')}
    del _L0_gnn_all

    def _L1_gnn_setup():
        import jax, jax.numpy as jnp
        import numpy as np
        N_NODES = 6250

        def _gcn_conv(x, row, col, W, b, n_nodes):
            h = x @ W
            deg = jax.ops.segment_sum(jnp.ones(col.shape[0], x.dtype), col, num_segments=n_nodes)
            dis = jnp.where(deg > 0, jax.lax.rsqrt(deg), 0.0)
            norm = dis[row] * dis[col]
            msg = h[row] * norm[:, None]
            out = jax.ops.segment_sum(msg, col, num_segments=n_nodes)
            return out + b
        key = jax.random.key(seed)
        k1, k2, k3, k4 = jax.random.split(key, 4)
        N, E, FIN, FH = (N_NODES, 100000, 512, 512)
        x = jax.random.normal(k1, (N, FIN), dtype=jnp.float32)
        edge_index = jax.random.randint(k2, (2, E), 0, N, dtype=jnp.int64)
        W1 = jax.random.normal(k3, (FIN, FH), dtype=jnp.float32) * (1.0 / np.sqrt(FIN))
        b1 = jnp.zeros((FH,), jnp.float32)
        W2 = jax.random.normal(k4, (FH, FH), dtype=jnp.float32) * (1.0 / np.sqrt(FH))
        b2 = jnp.zeros((FH,), jnp.float32)
        return {'x': x, 'edge_index': edge_index, 'W1': W1, 'b1': b1, 'W2': W2, 'b2': b2}
    _L1_gnn_all = _L1_gnn_setup()
    _L1_gnn_in = {k: v for k, v in _L1_gnn_all.items() if k in ('W1', 'b1', 'W2', 'b2')}
    del _L1_gnn_all
    return {'x': x, 'src': src, 'dst': dst, 'edge_weight': edge_weight, 'L0_gnn_W_gcn': _L0_gnn_in['W_gcn'], 'L0_gnn_b_gcn': _L0_gnn_in['b_gcn'], 'L0_gnn_W_mlp': _L0_gnn_in['W_mlp'], 'L0_gnn_b_mlp': _L0_gnn_in['b_mlp'], 'L1_gnn_W1': _L1_gnn_in['W1'], 'L1_gnn_b1': _L1_gnn_in['b1'], 'L1_gnn_W2': _L1_gnn_in['W2'], 'L1_gnn_b2': _L1_gnn_in['b2']}

def reference(x, src, dst, edge_weight, L0_gnn_W_gcn, L0_gnn_b_gcn, L0_gnn_W_mlp, L0_gnn_b_mlp, L1_gnn_W1, L1_gnn_b1, L1_gnn_W2, L1_gnn_b2):
    import jax
    import jax.numpy as jnp

    def _L0_gnn_ref(x, edge_weights, W_gcn, b_gcn, W_mlp, b_mlp, edge_index):
        import jax, jax.numpy as jnp
        import numpy as np
        N_NODES = 1024
        D_MODEL = 512
        N_LAYERS = 2
        N_EDGES = 32768
        LEAKY_SLOPE = 0.01

        def _normalized_adj(edge_index, edge_weights, num_nodes):
            A = jnp.zeros((num_nodes, num_nodes), dtype=edge_weights.dtype)
            A = A.at[edge_index[0], edge_index[1]].add(edge_weights)
            deg = jnp.sum(A, axis=1)
            dinv = jnp.where(deg > 0, deg ** (-0.5), 0.0)
            return dinv[:, None] * A * dinv[None, :]
        N = x.shape[0]
        A_norm = _normalized_adj(edge_index, edge_weights, N)
        h = x
        for l in range(W_gcn.shape[0]):
            h = A_norm @ h
            h = h @ W_gcn[l] + b_gcn[l]
            h = jax.nn.leaky_relu(h @ W_mlp[l] + b_mlp[l], negative_slope=LEAKY_SLOPE)
        return h

    def _L1_gnn_ref(x, edge_index, W1, b1, W2, b2):
        import jax, jax.numpy as jnp
        import numpy as np
        N_NODES = 6250

        def _gcn_conv(x, row, col, W, b, n_nodes):
            h = x @ W
            deg = jax.ops.segment_sum(jnp.ones(col.shape[0], x.dtype), col, num_segments=n_nodes)
            dis = jnp.where(deg > 0, jax.lax.rsqrt(deg), 0.0)
            norm = dis[row] * dis[col]
            msg = h[row] * norm[:, None]
            out = jax.ops.segment_sum(msg, col, num_segments=n_nodes)
            return out + b
        n = x.shape[0]
        loops = jnp.arange(n, dtype=edge_index.dtype)
        row = jnp.concatenate([edge_index[0], loops])
        col = jnp.concatenate([edge_index[1], loops])
        h = _gcn_conv(x, row, col, W1, b1, n)
        h = jax.nn.relu(h)
        return _gcn_conv(h, row, col, W2, b2, n)
    edge_index = jnp.stack([src, dst])
    x = _layernorm(x + _L0_gnn_ref(x, edge_weight, L0_gnn_W_gcn, L0_gnn_b_gcn, L0_gnn_W_mlp, L0_gnn_b_mlp, edge_index), axis=-1)
    x = _layernorm(x + _L1_gnn_ref(x, edge_index, L1_gnn_W1, L1_gnn_b1, L1_gnn_W2, L1_gnn_b2), axis=-1)
    return x

_drawn_inputs = setup_inputs


def setup_inputs(seed=0):
    import zlib

    import numpy as np

    out = dict(_drawn_inputs(seed))
    spreads = {'L0_gnn_b_gcn': (0.0, 0.1),
     'L0_gnn_b_mlp': (0.0, 0.1),
     'L1_gnn_b1': (0.0, 0.1),
     'L1_gnn_b2': (0.0, 0.1)}
    factors = {'edge_weight': 8.0, 'L0_gnn_W_gcn': 4.571}
    for name, (base, spread) in spreads.items():
        noise = np.random.default_rng([zlib.crc32(name.encode()), seed]).standard_normal(out[name].shape)
        drawn = base * np.exp(spread * noise) if base else spread * noise
        out[name] = jnp.asarray(drawn.astype(out[name].dtype))
    for name, factor in factors.items():
        out[name] = (out[name] * factor).astype(out[name].dtype)
    return out
```

```python
from contextlib import ExitStack

import concourse.bass as bass
from concourse import mybir

F32 = mybir.dt.float32
F32R = mybir.dt.float32r
I32 = mybir.dt.int32
ALU = mybir.AluOpType
ACT = mybir.ActivationFunctionType
AX = mybir.AxisListType

P = 128
BANK = 512
WINDOW = 12
G = 4
SLOPE = 0.01
EPS = 1e-5
PREP_TURN = 13
N_CONSTS = 4
FULL = False
EXACT_DEGREE = 4000.0


def gnn_resnorm(nc, x, src, dst, weight, wg, bg, wm, bm, w1, b1, w2, b2, out):
    N, D = x.shape
    E = src.shape[0]
    NB = N // P
    KD = D // P
    CH = E // P
    NG = CH // G
    WC = WINDOW * NB
    HALF = NB // 2
    assert D == BANK and CH == P and N * 1 == 2 * BANK and NB == 8 and KD == 4

    with ExitStack() as ctx:
        start = (nc.sbuf_base + 31) // 32 * 32
        KB = 1024
        ADJ, ATH, YR, HR, XR, WR, SM = (start + k * KB for k in (0, 64, 96, 128, 160, 176, 192))
        cursor = {}

        def at(name, region, shape, dtype):
            size = 4
            for n in shape[1:]:
                size *= n
            offset = cursor.get(region, region)
            cursor[region] = offset + (size + 31) // 32 * 32
            return nc.alloc_sbuf_tensor_at(name, shape, dtype, offset=offset)

        def again(region):
            cursor[region] = region

        adj = at("adj", ADJ, [P, 2, N * NB], F32)
        again(ADJ)
        at_low = at("at_low", ADJ, [P, NB, N], F32R)
        sel = at("sel", ATH, [P, 2, G, P], F32R)
        hot = at("hot", ATH, [P, 2, G, 4, WC], F32R)
        ramp = at("ramp", ATH, [P, BANK], F32)
        tables = at("tables", ATH, [P, 6, P], F32)
        wg_raw = at("wg_raw", ATH, [P, KD, D], F32)
        bias_rows = at("bias_rows", ATH, [3, D], F32)
        ones3 = at("ones3", ATH, [3, P], F32)
        bg_raw = at("bg_raw", ATH, [P, KD], F32)
        bg_parts = at("bg_parts", ATH, [P, KD, 2], F32R)
        assert cursor[ATH] <= YR
        again(ATH)
        at_high = at("at_high", ATH, [P, NB, NB, P], F32R)
        again(ATH)
        cnt = at("cnt", ATH, [P, NB, NB, P], F32R)
        wgt_high = at("wgt_high", YR, [P, KD, D], F32R)
        wgt_low = at("wgt_low", YR, [P, KD, D], F32R)
        wm_high = at("wm_high", YR, [P, KD, D], F32R)
        wm_raw = at("wm_raw", YR, [P, KD, D], F32)
        cursor[YR] -= 4 * KD * D
        wm_low = at("wm_low", YR, [P, KD, D], F32R)
        again(YR)
        y_high = at("y_high", YR, [P, NB, D], F32R)
        y_low = at("y_low", YR, [P, NB, D], F32R)
        ht_high = at("ht_high", HR, [P, KD, N], F32R)
        ht_low = at("ht_low", HR, [P, KD, N], F32R)
        x_first = at("x_first", XR, [P, NB, D], F32)
        again(XR)
        wcb_high = at("wcb_high", XR, [P, KD, D], F32R)
        wcb_low = at("wcb_low", XR, [P, KD, D], F32R)
        again(XR)
        xs = at("xs", XR, [P, NB, D], F32)
        wca_high = at("wca_high", WR, [P, KD, D], F32R)
        wca_low = at("wca_low", WR, [P, KD, D], F32R)
        again(WR)
        cnt_sums = at("cnt_sums", WR, [P, N], F32)
        ones_mat = at("ones_mat", WR, [P, 2], F32)
        again(WR)
        w12_high = at("w12_high", WR, [P, KD, D], F32R)
        w12_raw = at("w12_raw", WR, [P, KD, D], F32)
        cursor[WR] -= 4 * KD * D
        w12_low = at("w12_low", WR, [P, KD, D], F32R)
        tmp = at("tmp", SM, [P, 3, BANK], F32)
        col_scale = at("col_scale", SM, [P, N], F32)
        bias_bc = at("bias_bc", SM, [P, 2, D], F32)
        ident = at("ident", SM, [P, P], F32)
        base_row = at("base_row", SM, [1, P], I32)
        small = at("small", SM, [P, 112], F32)
        flags = at("flags", SM, [1, 8], I32)
        assert cursor[SM] <= nc.sbuf_usable_end, (cursor[SM], nc.sbuf_usable_end)
        EDGE = start + 192 * KB + 4 * 3 * BANK
        src_i = at("src_i", EDGE, [P, P], I32)
        dst_i = at("dst_i", EDGE, [P, P], I32)
        w_e = at("w_e", EDGE, [P, P], F32)
        dst_f = at("dst_f", EDGE, [P, P], F32)
        hi_i = at("hi_i", EDGE, [P, P], I32)
        lo_i = at("lo_i", EDGE, [P, P], I32)
        hi_f = at("hi_f", EDGE, [P, P], F32)
        lo_f = at("lo_f", EDGE, [P, P], F32)
        col_f = at("col_f", EDGE, [P, P], F32)
        w_high = at("w_high", EDGE, [P, P], F32R)
        w_low = at("w_low", EDGE, [P, P], F32)
        assert cursor[EDGE] <= EDGE + 8 * KB

        deg = small[:, 0:8]
        dinv = small[:, 8:16]
        dis = small[:, 16:24]
        power = small[:, 24:32]
        deg_pos = small[:, 32:40]
        deg_safe = small[:, 40:48]
        base_max = small[:, 48:50]
        pidx = small[:, 50:51]
        bias_t = small[:, 52:56]
        b1_t = small[:, 56:60]
        stats = small[:, 60:72]
        mean_var = small[:, 72:76]
        rstd = small[:, 76:80]
        overflow = small[:, 80:81]
        deg1 = small[:, 84:92]
        max_col = small[0:1, 100:101]

        win = ctx.enter_context(nc.psum_tensor("win", [P, 2, G, 256], F32))
        work = ctx.enter_context(nc.psum_tensor("work", [P, 4, BANK], F32))
        WB = 4

        SCALAR, VECTOR = "scalar", "vector"
        tiles = [("tab", 0, VECTOR), ("tab", 1, VECTOR)]
        first_fill = len(tiles)
        for l in (0, 1):
            tiles += [(f"wgt{l}", k, SCALAR) for k in range(KD)]
            if l == 0:
                tiles += [("xt", b, SCALAR) for b in range(NB)]
            tiles += [(f"bias{l}", 0, SCALAR)] + [(f"wc{l}", k, SCALAR) for k in range(KD)]
            tiles += [(f"biasb{l}", 0, SCALAR)]
        fills = tiles[first_fill:]
        tiles += [("y0", b, SCALAR) for b in range(NB)]
        tiles += [("dinvb", h, VECTOR) for h in range(2)]
        tiles += [("at", 2 * j + h, VECTOR) for j in range(NB) for h in range(2)]
        tiles += [("h1", f, VECTOR) for f in range(2 * KD)]
        tiles += [("deg1", 0, VECTOR)]
        tiles += [("y1", b, VECTOR) for b in range(NB)]
        tiles += [("disb", h, VECTOR) for h in range(2)]
        tiles += [("h2", 0, VECTOR)]
        for b in range(1, NB):
            tiles += [("h2", b, VECTOR), ("x1t", b - 1, VECTOR)]
        tiles += [("y2", b, VECTOR) for b in range(NB - 1)] + [("x1t", NB - 1, VECTOR)]
        tiles += [("y2", NB - 1, VECTOR)]
        tiles += [("h3", f, VECTOR) for f in range(2 * KD)]
        tiles += [("y3", b, VECTOR) for b in range(NB)]
        tiles += [("h4", b, VECTOR) for b in range(NB)]
        index = {t[:2]: n for n, t in enumerate(tiles)}
        done_at, freed = {}, {SCALAR: 0, VECTOR: 0}
        for n, t in enumerate(tiles):
            freed[t[2]] += 1
            done_at[n] = (t[2], freed[t[2]])

        def read(eng, name, i=0):
            who, value = done_at[index[(name, i)]]
            eng.wait_ge(scalar_freed if who == SCALAR else vector_freed, value)

        def bank(name, i=0):
            return work[:, index[(name, i)] % WB, :]

        sem = lambda name: ctx.enter_context(nc.semaphore(name))
        edges_in = sem("edges_in")
        x_in, x_again_in = sem("x_in"), sem("x_again_in")
        wg_in, wm_in = sem("wg_in"), sem("wm_in")
        bg_in, bm_in = sem("bg_in"), sem("bm_in")
        b1_in, b2_in = sem("b1_in"), sem("b2_in")
        w1_in, w2_in = sem("w1_in"), sem("w2_in")
        consts = sem("consts")
        zeros = sem("zeros")
        prep = sem("prep")
        tile_done = sem("tile_done")
        scalar_freed = sem("scalar_freed")
        vector_freed = sem("vector_freed")
        sel_ready = sem("sel_ready")
        hot_ready = sem("hot_ready")
        whigh_ready = sem("whigh_ready")
        wlow_ready = sem("wlow_ready")
        group_done = sem("group_done")
        added = sem("added")
        adj_ready = sem("adj_ready")
        gen_ready, gen_done, gen_added = sem("gen_ready"), sem("gen_done"), sem("gen_added")
        gen_mask = sem("gen_mask")
        split_copy = sem("split_copy")
        split_low = sem("split_low")
        wm_split_high, wm_split_low = sem("wm_split_high"), sem("wm_split_low")
        bg_high, bg_split = sem("bg_high"), sem("bg_split")
        deg_ready = sem("deg_ready")
        pow_ready = sem("pow_ready")
        dinv_ready = sem("dinv_ready")
        high_ready = sem("high_ready")
        sums_ready = sem("sums_ready")
        ones_ready = sem("ones_ready")
        row_biased, row_leaked = sem("row_biased"), sem("row_leaked")
        row_high, row_low = sem("row_high"), sem("row_low")
        norm = sem("norm")
        var_ready, rstd_ready = sem("var_ready"), sem("rstd_ready")
        x1_ready = sem("x1_ready")
        cnt_ready = sem("cnt_ready")
        overflow_ready = sem("overflow_ready")
        w1_high, w1_low, w2_high, w2_low = sem("w1_high"), sem("w1_low"), sem("w2_high"), sem("w2_low")
        out_ready, stored = sem("out_ready"), sem("stored")

        FILLS = len(fills)
        is_split = [not t[0].startswith("bias") for t in fills] + [True] * NB
        p1 = fills + [("y0", b, SCALAR) for b in range(NB)]
        split_count = {}
        for n, t in enumerate(p1):
            split_count[t[:2]] = sum(is_split[:n + 1])

        def parts_of(t):
            name, i = t[0], t[1]
            if name.startswith("wgt"):
                return wgt_high[:, i, :], wgt_low[:, i, :]
            if name == "xt":
                return (ht_high[:, :, i * P:(i + 1) * P], ht_low[:, :, i * P:(i + 1) * P])
            if name == "wc0":
                return wca_high[:, i, :], wca_low[:, i, :]
            if name == "wc1":
                return wcb_high[:, i, :], wcb_low[:, i, :]
            return y_high[:, i, :], y_low[:, i, :]

        def shaped(ap, name):
            return ap.rearrange("p (k n) -> p k n", k=KD) if name in ("xt", "x1t") else ap

        hot_flat = hot[:].rearrange("p a g b c -> p (a g b c)")
        block = ctx.enter_context(nc.Block())

        @block.sync
        def _(sp):
            rows = "(c e) -> c e"
            sp.dma_start(dst_i[:], dst.rearrange(rows, e=P)).then_inc(edges_in, 16)
            sp.dma_start(src_i[:], src.rearrange(rows, e=P)).then_inc(edges_in, 16)
            sp.dma_start(w_e[:], weight.rearrange(rows, e=P)).then_inc(edges_in, 16)
            by_k = "(k p) n -> p k n"
            sp.dma_start(wg_raw[:], wg[0].rearrange(by_k, p=P)).then_inc(wg_in, 16)
            sp.dma_start(x_first[:], x.rearrange(by_k, p=P)).then_inc(x_in, 16)
            sp.dma_start(wm_raw[:], wm[0].rearrange(by_k, p=P)).then_inc(wm_in, 16)
            with nc.allow_non_contiguous_dma(reason="bias columns"):
                sp.dma_start(bg_raw[:], bg[0].rearrange("(k p) -> p k", p=P)).then_inc(bg_in, 16)
                sp.dma_start(b1_t, b1.rearrange("(k p) -> p k", p=P)).then_inc(b1_in, 16)
            sp.dma_start(bias_rows[2:3, :], bm[0:1, :]).then_inc(bm_in, 16)
            sp.wait_ge(tile_done, index[("wgt0", KD - 1)] + 1)
            sp.dma_start(wg_raw[:], wg[1].rearrange(by_k, p=P)).then_inc(wg_in, 16)
            sp.wait_ge(bg_split, 1)
            with nc.allow_non_contiguous_dma(reason="bias columns"):
                sp.dma_start(bg_raw[:], bg[1].rearrange("(k p) -> p k", p=P)).then_inc(bg_in, 16)
            sp.wait_ge(tile_done, index[("wc0", KD - 1)] + 1)
            sp.dma_start(wm_raw[:], wm[1].rearrange(by_k, p=P)).then_inc(wm_in, 16)
            sp.wait_ge(tile_done, index[("biasb0", 0)] + 1)
            sp.dma_start(bias_rows[2:3, :], bm[1:2, :]).then_inc(bm_in, 16)
            sp.wait_ge(vector_freed, 2)
            sp.dma_start(bias_bc[:, 1, :], b2.rearrange("(a n) -> a n", a=1).broadcast_to([P, D])).then_inc(b2_in, 16)
            sp.wait_ge(tile_done, index[("deg1", 0)] + 1)
            sp.dma_start(w12_raw[:], w1.rearrange(by_k, p=P)).then_inc(w1_in, 16)
            sp.wait_ge(tile_done, index[("y1", NB - 1)] + 1)
            sp.dma_start(xs[:], x.rearrange(by_k, p=P)).then_inc(x_again_in, 16)
            sp.wait_ge(tile_done, index[("y2", NB - 1)] + 1)
            sp.dma_start(w12_raw[:], w2.rearrange(by_k, p=P)).then_inc(w2_in, 16)
            for b in range(NB):
                sp.wait_ge(out_ready, b + 1)
                sp.dma_start(out[b * P:(b + 1) * P, :], xs[:, b, :]).then_inc(stored, 16)
            sp.wait_ge(stored, 16 * NB)

        @block.gpsimd
        def _(pool):
            pool.iota(ramp[:], [[1, BANK]], base=0, channel_multiplier=0,
                      allow_small_or_imprecise_dtypes=True).then_inc(consts, 1)
            pool.iota(pidx, [[0, 1]], base=0, channel_multiplier=1,
                      allow_small_or_imprecise_dtypes=True).then_inc(consts, 1)
            pool.memset(power, -0.5).then_inc(consts, 1)
            pool.memset(ones3[:], 1.0).then_inc(consts, 1)
            pool.memset(hot[:, :, :, 3, :].bitcast(F32), 0.0).then_inc(zeros, 1)
            pool.memset(adj[:, 1, :], 0.0).then_inc(zeros, 1)
            pool.memset(adj[:, 0, 0:3 * N], 0.0).then_inc(zeros, 1)

            def weigh(g):
                pool.wait_ge(hot_ready, g + 1)
                w = tables[:, 2, g * G:(g + 1) * G].unsqueeze(2).broadcast_to([P, G, WC])
                pool.tensor_tensor(hot[:, g % 2, :, 0, :], hot[:, g % 2, :, 1, :].bitcast(F32), w,
                                   ALU.mult).then_inc(whigh_ready, 1)

            def low(t):
                n = split_count[t[:2]]
                read(pool, *t[:2])
                hi, lo = parts_of(t)
                pool.tensor_tensor(lo, shaped(tmp[:, n % 2, :], t[0]), hi.bitcast(F32),
                                   ALU.subtract).then_inc(split_low, 1)

            def wm_lower(l):
                pool.wait_ge(bg_in, 16 * (l + 1))
                if l == 1:
                    pool.wait_ge(tile_done, index[("bias0", 0)] + 1)
                pool.tensor_copy(bg_parts[:, :, 0], bg_raw[:]).then_inc(bg_high, 1)
                pool.wait_ge(bg_high, l + 1)
                pool.tensor_tensor(bg_parts[:, :, 1], bg_raw[:], bg_parts[:, :, 0].bitcast(F32),
                                   ALU.subtract).then_inc(bg_split, 1)
                pool.wait_ge(wm_split_high, l + 1)
                pool.tensor_tensor(wm_low[:], wm_raw[:], wm_high[:].bitcast(F32),
                                   ALU.subtract).then_inc(wm_split_low, 1)

            pool.wait_ge(consts, N_CONSTS)
            pool.wait_ge(vector_freed, 2)
            weigh(0)
            wm_lower(0)
            for n in range(NG - 1 + NB):
                if n + 1 < NG:
                    weigh(n + 1)
                if n >= NG - 1:
                    low(p1[n - NG + 1 + FILLS])
                elif n < FILLS:
                    if p1[n][0] == "wgt1" and p1[n][1] == KD - 1:
                        low(p1[n])
                        wm_lower(1)
                    elif is_split[n]:
                        low(p1[n])

            def to_power(safe, res, count):
                pool.tensor_tensor(res, safe, power[:, 0:count], ALU.pow).then_inc(pow_ready, 1)

            pool.wait_ge(deg_ready, 1)
            to_power(deg_safe, dinv, NB)
            n_rows = [0]

            def row_lower(dest, high):
                n_rows[0] += 1
                n = n_rows[0]
                pool.wait_ge(row_high, n)
                pool.tensor_tensor(dest, tmp[:, (n - 1) % 3, :], high.bitcast(F32),
                                   ALU.subtract).then_inc(row_low, 1)

            def w_lower(ready, high_sem):
                pool.wait_ge(high_sem, 1)
                pool.tensor_tensor(w12_low[:], w12_raw[:], w12_high[:].bitcast(F32),
                                   ALU.subtract).then_inc(ready, 1)

            for n in range(2 * KD):
                h, f = divmod(n, KD)
                row_lower(ht_low[:, f, h * BANK:(h + 1) * BANK], ht_high[:, f, h * BANK:(h + 1) * BANK])
            read(pool, "deg1")
            to_power(deg1, dis, NB)
            w_lower(w1_low, w1_high)
            for b in range(NB):
                pool.wait_ge(var_ready, b + 1)
                r = rstd[:, 2 * (b % 2):2 * (b % 2) + 2]
                pool.tensor_tensor(r[:, 1:2], r[:, 0:1], power[:, 0:1], ALU.pow).then_inc(rstd_ready, 1)
                pool.wait_ge(tile_done, index[("h2", b)] + 1)
                block_of = adj[:, 1, b * P * NB:(b + 1) * P * NB].rearrange("p (d h) -> p h d", h=NB)
                if b > 0:
                    pool.tensor_copy(cnt[:, b, 0:b, :], block_of[:, 0:b, :]).then_inc(cnt_ready, 1)
                if b < NB - 1:
                    pool.tensor_copy(cnt[:, b, b + 1:NB, :], block_of[:, b + 1:NB, :]).then_inc(cnt_ready, 1)
                pool.tensor_tensor(cnt[:, b, b, :], block_of[:, b, :], ident[:], ALU.add).then_inc(cnt_ready, 1)
            for n in range(2 * KD):
                h, f = divmod(n, KD)
                row_lower(ht_low[:, f, h * BANK:(h + 1) * BANK], ht_high[:, f, h * BANK:(h + 1) * BANK])
                if n == 2:
                    w_lower(w2_low, w2_high)
            for b in range(NB):
                pool.wait_ge(var_ready, NB + b + 1)
                r = rstd[:, 2 * (b % 2):2 * (b % 2) + 2]
                pool.tensor_tensor(r[:, 1:2], r[:, 0:1], power[:, 0:1], ALU.pow).then_inc(rstd_ready, 1)

        @block.scalar
        def _(act):
            def weigh_low(g):
                act.wait_ge(hot_ready, g + 1)
                for j in range(G):
                    c = g * G + j
                    ins = act.activation(hot[:, g % 2, j, 2, :], hot[:, g % 2, j, 1, :].bitcast(F32), ACT.Copy,
                                         scale=tables[:, 3, c:c + 1])
                ins.then_inc(wlow_ready, 1)

            def wm_upper(l):
                act.wait_ge(wm_in, 16 * (l + 1))
                act.activation(wm_high[:], wm_raw[:], ACT.Copy).then_inc(wm_split_high, 1)

            def fill(t):
                name, i = t[0], t[1]
                act.wait_ge(tile_done, index[(name, i)] + 1)
                if name.startswith("bias"):
                    l = int(name[-1])
                    if not name.startswith("biasb"):
                        act.activation(bias_rows[0:2, :], bank(name)[0:2, :], ACT.Copy).then_inc(scalar_freed, 1)
                    elif l == 0:
                        act.activation(bias_t, bank(name)[:, 0:KD], ACT.Copy).then_inc(scalar_freed, 1)
                    else:
                        act.activation(bias_bc[:, 0, :], bank(name), ACT.Copy).then_inc(scalar_freed, 1)
                    return
                n = split_count[(name, i)]
                if n > 2:
                    act.wait_ge(split_low, n - 2)
                hi, lo = parts_of(t)
                if name.startswith("y0") and i == 0:
                    act.wait_ge(wm_split_low, 2)
                act.activation(tmp[:, n % 2, :], bank(name, i), ACT.Copy).then_inc(split_copy, 1)
                act.activation(hi, shaped(bank(name, i), name), ACT.Copy).then_inc(scalar_freed, 1)

            wm_upper(0)
            act.wait_ge(vector_freed, 2)
            weigh_low(0)
            for n in range(NG - 1 + NB):
                if n + 1 < NG:
                    weigh_low(n + 1)
                if n >= NG - 1:
                    fill(p1[n - NG + 1 + FILLS])
                elif n < FILLS:
                    fill(p1[n])
                    if p1[n][:2] == ("wgt1", KD - 1):
                        wm_upper(1)

            def upper(name, i, dest, scale=None):
                act.wait_ge(tile_done, index[(name, i)] + 1)
                kw = {} if scale is None else {"scale": scale}
                act.activation(dest, shaped(bank(name, i), name), ACT.Copy, **kw).then_inc(high_ready, 1)

            act.wait_ge(dinv_ready, 1)
            for n in range(2 * NB):
                j, h = divmod(n, 2)
                act.wait_ge(tile_done, index[("at", n)] + 1)
                act.activation(at_high[:, h * HALF:(h + 1) * HALF, j, :],
                               bank("at", n).rearrange("p (b n) -> p b n", b=HALF), ACT.Copy,
                               scale=dinv[:, j:j + 1]).then_inc(high_ready, 1)

            n_rows = [0]

            def row_steps(bias, f, h, leaky):
                n_rows[0] += 1
                n = n_rows[0]
                row = tmp[:, (n - 1) % 3, :]
                read(act, "h1" if leaky else "h3", h * KD + f)
                act.activation(row, row, ACT.Identity if leaky else ACT.Relu, bias=bias[:, f:f + 1])\
                    .then_inc(row_biased, 1)
                if leaky:
                    act.wait_ge(row_leaked, n)
                else:
                    act.wait_ge(row_biased, n)
                act.activation(ht_high[:, f, h * BANK:(h + 1) * BANK], row, ACT.Copy).then_inc(row_high, 1)

            for n in range(2 * KD):
                h, f = divmod(n, KD)
                row_steps(bias_t, f, h, True)
            for b in range(NB):
                upper("y1", b, y_high[:, b, :])
            act.wait_ge(w1_in, 16)
            act.activation(w12_high[:], w12_raw[:], ACT.Copy).then_inc(w1_high, 1)
            for name, i, _ in tiles[index[("x1t", 0)]:index[("y2", NB - 1)] + 1]:
                if name == "x1t":
                    upper(name, i, ht_high[:, :, i * P:(i + 1) * P])
                elif name == "y2":
                    upper(name, i, y_high[:, i, :], dis[:, i:i + 1])
            for n in range(2 * KD):
                h, f = divmod(n, KD)
                row_steps(b1_t, f, h, False)
                if n == 2:
                    act.wait_ge(w2_in, 16)
                    act.activation(w12_high[:], w12_raw[:], ACT.Copy).then_inc(w2_high, 1)
            for b in range(NB):
                upper("y3", b, y_high[:, b, :], dis[:, b:b + 1])

        @block.tensor
        def _(pe):
            state = {"n": 0}

            def begin(name, i=0):
                n = index[(name, i)]
                assert n == state["n"], (name, i, n, state["n"])
                state["n"] += 1
                if n >= WB:
                    read(pe, *tiles[n - WB][:2])
                return work[:, n % WB, :]

            def split_product(dest, stationary, moving, both_low=False):
                pairs = []
                for (sh, sl), (mh, ml) in zip(stationary, moving):
                    pairs += [(sh, mh)]
                    if sl is not None:
                        pairs += [(sl, mh)]
                    if ml is not None:
                        pairs += [(sh, ml)]
                    if sl is not None and ml is not None and FULL:
                        pairs += [(sl, ml)]
                for n, (s, m) in enumerate(pairs):
                    ins = pe.matmul(dest, s, m, start=(n == 0), stop=(n == len(pairs) - 1))
                return ins

            def turn(dest, blocks):
                for n, b in enumerate(blocks):
                    ins = pe.transpose(dest[:, n * P:(n + 1) * P], b, ident[:])
                return ins

            def group(g):
                pe.wait_ge(sel_ready, g + 1)
                pe.wait_ge(whigh_ready, g + 1)
                pe.wait_ge(wlow_ready, g + 1)
                if g >= 2:
                    pe.wait_ge(added, 1 + G * (g - 1))
                for j in range(G):
                    for part in (0, 2):
                        ins = pe.matmul(win[:, g % 2, j, 0:2 * WC], sel[:, g % 2, j, :],
                                        hot[:, g % 2, j, part:part + 2, :].rearrange("p a b -> p (a b)"),
                                        start=(part == 0), stop=(part == 2))
                ins.then_inc(group_done, 1)

            def kblocks(high, low, f=None):
                cut = (lambda a, k: a[:, k, f * P:(f + 1) * P]) if f is not None else (lambda a, k: a[:, k, :])
                return [(cut(high, k), cut(low, k)) for k in range(KD)]

            def filler(t):
                name, i = t[0], t[1]
                b = begin(name, i)
                if name.startswith("wgt"):
                    l = int(name[-1])
                    if i == 0:
                        pe.wait_ge(wg_in, 16 * (l + 1))
                    ins = turn(b, [wg_raw[:, m, i * P:(i + 1) * P] for m in range(KD)])
                elif name == "xt":
                    if i == 0:
                        pe.wait_ge(x_in, 16)
                    ins = turn(b, [x_first[:, i, k * P:(k + 1) * P] for k in range(KD)])
                elif name.startswith("wc"):
                    l = int(name[-1])
                    if i == 0:
                        pe.wait_ge(wm_split_low, l + 1)
                        pe.wait_ge(split_low, split_count[(f"wgt{l}", KD - 1)])
                    ins = split_product(b, kblocks(wgt_high, wgt_low, i), kblocks(wm_high, wm_low))
                elif name.startswith("biasb"):
                    l = int(name[-1])
                    pe.wait_ge(bm_in, 16 * (l + 1))
                    read(pe, f"bias{l}")
                    if l == 0:
                        for f in range(KD):
                            ins = pe.matmul(b[:, f:f + 1], bias_rows[:, f * P:(f + 1) * P], ones3[:, 0:1],
                                            start=True, stop=True)
                    else:
                        ins = pe.matmul(b, ones3[:], bias_rows[:], start=True, stop=True)
                else:
                    l = int(name[-1])
                    pe.wait_ge(bg_split, l + 1)
                    pe.wait_ge(wm_split_low, l + 1)
                    ops = [(bg_parts[:, k, :], m[:, k, :]) for k in range(KD) for m in (wm_high, wm_low)]
                    for n, (s, m) in enumerate(ops):
                        ins = pe.matmul(b[0:2, :], s, m, start=(n == 0), stop=(n == len(ops) - 1))
                ins.then_inc(tile_done, 1)

            pe.wait_ge(consts, N_CONSTS)
            pe.wait_ge(prep, PREP_TURN)
            b = begin("tab", 0)
            turn(b, [col_f[:]]).then_inc(group_done, 1)
            turn(b[:, P:], [lo_f[:], w_high[:].bitcast(F32), w_low[:]]).then_inc(tile_done, 1)
            b = begin("tab", 1)
            turn(b, [dst_f[:], hi_f[:]])
            for n in range(2):
                ins = pe.transpose(b[0:1, (2 + n) * P:(3 + n) * P], base_max[:, n:n + 1], ident[:])
            ins.then_inc(tile_done, 1)

            assert FILLS < NG
            for n in range(NG):
                group(n)
                if n < FILLS:
                    filler(fills[n])

            uncovered = pe.value_load(flags[0:1, 0:1], min_val=0, max_val=1)
            with pe.If(uncovered > 0):
                with pe.Fori(0, 2 * NB) as t:
                    with pe.Fori(0, CH) as c:
                        pe.wait_ge(gen_ready, t * CH + c + 1)
                        first = win[:, 0, 0:2, :].rearrange("p a b -> p (a b)")
                        second = win[:, 0, 2:4, :].rearrange("p a b -> p (a b)")
                        gen_m = hot_flat[:, 0:3 * BANK]
                        pe.matmul(first, sel[:, 0, 0, :], gen_m[:, 0:BANK], start=True, stop=False)
                        pe.matmul(first, sel[:, 0, 0, :], gen_m[:, BANK:2 * BANK], start=False, stop=True)
                        pe.matmul(second, sel[:, 0, 0, :], gen_m[:, 2 * BANK:3 * BANK], start=True, stop=True)\
                            .then_inc(gen_done, 1)
            with pe.Else():
                pe.nop()

            def y_tile(name, i, high, low):
                return split_product(begin(name, i),
                                     [(ht_high[:, k, i * P:(i + 1) * P], ht_low[:, k, i * P:(i + 1) * P])
                                      for k in range(KD)],
                                     kblocks(high, low))

            pe.wait_ge(split_low, split_count[("wc1", KD - 1)])
            for i in range(NB):
                y_tile("y0", i, wca_high, wca_low).then_inc(tile_done, 1)

            def spread(name, h, scales):
                b = begin(name, h)
                for n in range(HALF):
                    hb = h * HALF + n
                    ins = pe.matmul(b[:, n * P:(n + 1) * P], scales[:, hb:hb + 1].broadcast_to([P, P]), ident[:],
                                    start=True, stop=True)
                ins.then_inc(tile_done, 1)

            pe.wait_ge(dinv_ready, 1)
            for h in range(2):
                spread("dinvb", h, dinv)
            pe.wait_ge(adj_ready, 1)
            for n in range(2 * NB):
                j, h = divmod(n, 2)
                b = begin("at", n)
                blocks = [adj[:, 0, j * P * NB + hb:(j + 1) * P * NB:NB] for hb in range(h * HALF, (h + 1) * HALF)]
                turn(b, blocks).then_inc(tile_done, 1)

            pe.wait_ge(split_low, split_count[("y0", NB - 1)])
            read(pe, "at", 2 * NB - 1)
            for n in range(2 * KD):
                h, f = divmod(n, KD)
                split_product(begin("h1", n),
                              [(y_high[:, j, f * P:(f + 1) * P], y_low[:, j, f * P:(f + 1) * P])
                               for j in range(NB)],
                              [(at_high[:, h * HALF:(h + 1) * HALF, j, :], at_low[:, j, h * BANK:(h + 1) * BANK])
                               for j in range(NB)]).then_inc(tile_done, 1)
            pe.wait_ge(sums_ready, 1)
            b = begin("deg1")
            for n in range(NB):
                ins = pe.matmul(b[:, n:n + 1], cnt_sums[:, n * P:(n + 1) * P], ones_mat[:, 0:1],
                                start=True, stop=True)
            ins.then_inc(tile_done, 1)
            for i in range(NB):
                if i % HALF == 0:
                    pe.wait_ge(row_low, KD * (i // HALF + 1))
                y_tile("y1", i, wcb_high, wcb_low).then_inc(tile_done, 1)
            pe.wait_ge(pow_ready, 2)
            for h in range(2):
                spread("disb", h, dis)
            read(pe, "y1", NB - 1)

            def x1_turn(i):
                pe.wait_ge(x1_ready, i + 1)
                turn(begin("x1t", i), [xs[:, i, k * P:(k + 1) * P] for k in range(KD)]).then_inc(tile_done, 1)

            for i in range(NB):
                split_product(begin("h2", i),
                              [(at_high[:, i, j, :], at_low[:, j, i * P:(i + 1) * P]) for j in range(NB)],
                              [(y_high[:, j, :], y_low[:, j, :]) for j in range(NB)]).then_inc(tile_done, 1)
                if i > 0:
                    x1_turn(i - 1)
            pe.wait_ge(w1_low, 1)
            for i in range(NB):
                if i == NB - 1:
                    x1_turn(i)
                read(pe, "x1t", i)
                y_tile("y2", i, w12_high, w12_low).then_inc(tile_done, 1)
            pe.wait_ge(overflow_ready, 1)
            over = pe.value_load(flags[0:1, 1:2], min_val=0, max_val=1)
            pe.wait_ge(cnt_ready, 3 * NB - 2)
            read(pe, "y2", NB - 1)

            def counts_of(hb, d0, d1):
                return adj[:, 1, d0 * NB + hb:d1 * NB:NB]

            def h3(full):
                for n in range(2 * KD):
                    h, f = divmod(n, KD)
                    b = begin("h3", n) if not full else again_tile("h3", n)
                    s = [(y_high[:, j, f * P:(f + 1) * P], y_low[:, j, f * P:(f + 1) * P]) for j in range(NB)]
                    if not full:
                        split_product(b, s, [(cnt[:, h * HALF:(h + 1) * HALF, j, :], None) for j in range(NB)])\
                            .then_inc(tile_done, 1)
                        continue
                    ops = []
                    for j in range(NB):
                        for y in s[j]:
                            ops.append((b, y.bitcast(F32), counts_of(j, h * BANK, (h + 1) * BANK)))
                            if j // HALF == h:
                                c = (j % HALF) * P
                                ops.append((b[:, c:c + P], y.bitcast(F32), ident[:]))
                    for m, (d, s_, mv) in enumerate(ops):
                        ins = pe.matmul(d, s_, mv, start=(m == 0), stop=(m == len(ops) - 1),
                                        skip_group_check=True)
                    ins.then_inc(tile_done, 1)

            def h4(full):
                for i in range(NB):
                    b = begin("h4", i) if not full else again_tile("h4", i)
                    if not full:
                        split_product(b, [(cnt[:, i, j, :], None) for j in range(NB)],
                                      [(y_high[:, j, :], y_low[:, j, :]) for j in range(NB)])\
                            .then_inc(tile_done, 1)
                        continue
                    ops = []
                    for y in (y_high, y_low):
                        ops += [(counts_of(j, i * P, (i + 1) * P), y[:, j, :].bitcast(F32)) for j in range(NB)]
                        ops += [(ident[:], y[:, i, :].bitcast(F32))]
                    for m, (s_, mv) in enumerate(ops):
                        ins = pe.matmul(b, s_, mv, start=(m == 0), stop=(m == len(ops) - 1))
                    ins.then_inc(tile_done, 1)

            def again_tile(name, i):
                n = index[(name, i)]
                read(pe, *tiles[n - WB][:2])
                return work[:, n % WB, :]

            with pe.If(over > 0):
                h3(True)
            with pe.Else():
                h3(False)
            pe.wait_ge(w2_low, 1)
            for i in range(NB):
                if i % HALF == 0:
                    pe.wait_ge(row_low, 2 * KD + KD * (i // HALF + 1))
                y_tile("y3", i, w12_high, w12_low).then_inc(tile_done, 1)
            read(pe, "y3", NB - 1)
            with pe.If(over > 0):
                h4(True)
            with pe.Else():
                h4(False)

        @block.vector
        def _(dve):
            steps = {"prep": 0, "norm": 0}

            def chain(ins):
                steps["prep"] += 1
                ins.then_inc(prep, 1)
                return steps["prep"]

            dve.memset(adj[:, 0, 3 * N:NB * N], 0.0).then_inc(added, 1)
            dve.wait_ge(consts, N_CONSTS)
            chain(dve.tensor_scalar(ident[:], ramp[:, 0:P], pidx, None, ALU.is_equal))
            dve.wait_ge(edges_in, 48)
            chain(dve.tensor_copy(dst_f[:], dst_i[:]))
            chain(dve.tensor_scalar(hi_i[:], src_i[:], 7, None, ALU.arith_shift_right))
            chain(dve.tensor_scalar(lo_i[:], src_i[:], P - 1, None, ALU.bitwise_and))
            chain(dve.tensor_copy(w_high[:], w_e[:]))
            dve.wait_ge(prep, 2)
            chain(dve.tensor_reduce(base_max[:, 0:1], dst_f[:], AX.X, ALU.min))
            dve.wait_ge(prep, 4)
            chain(dve.tensor_copy(hi_f[:], hi_i[:]))
            chain(dve.tensor_copy(lo_f[:], lo_i[:]))
            dve.wait_ge(prep, 6)
            chain(dve.tensor_tensor(w_low[:], w_e[:], w_high[:].bitcast(F32), ALU.subtract))
            chain(dve.tensor_scalar(base_max[:, 0:1], base_max[:, 0:1], float(N - WINDOW), None, ALU.min))
            dve.wait_ge(prep, 10)
            chain(dve.tensor_scalar(col_f[:], dst_f[:], base_max[:, 0:1], float(NB),
                                    ALU.subtract, ALU.mult))
            dve.wait_ge(prep, 11)
            chain(dve.tensor_tensor(col_f[:], col_f[:], hi_f[:], ALU.add))
            dve.wait_ge(prep, 12)
            chain(dve.tensor_reduce(base_max[:, 1:2], col_f[:], AX.X, ALU.max))
            assert steps["prep"] == PREP_TURN
            dve.wait_ge(tile_done, 1)
            dve.tensor_copy(tables[:, 0:4, :].rearrange("p a b -> p (a b)"), bank("tab", 0)).then_inc(vector_freed, 1)
            dve.wait_ge(tile_done, 2)
            chain(dve.tensor_copy(tables[:, 4:6, :].rearrange("p a b -> p (a b)"), bank("tab", 1)[:, 0:2 * P]))
            chain(dve.tensor_scalar(base_row[:], bank("tab", 1)[0:1, 2 * P:3 * P], float(NB), None, ALU.mult))
            dve.tensor_reduce(max_col, bank("tab", 1)[0:1, 3 * P:4 * P], AX.X, ALU.max).then_inc(vector_freed, 1)
            dve.wait_ge(vector_freed, 2)
            chain(dve.tensor_scalar(flags[0:1, 0:1], max_col, float(WC), None, ALU.is_ge))
            dve.wait_ge(prep, steps["prep"])

            def make_sel(buf, cols):
                dve.tensor_tensor(sel[:, buf, :, :], ramp[:, 0:P].unsqueeze(1).broadcast_to([P, G, P]),
                                  tables[:, 1, cols].unsqueeze(2).broadcast_to([P, G, P]), ALU.is_equal)\
                    .then_inc(sel_ready, 1)

            def make_hot(buf, cols):
                dve.tensor_tensor(hot[:, buf, :, 1, :], ramp[:, 0:WC].unsqueeze(1).broadcast_to([P, G, WC]),
                                  tables[:, 0, cols].unsqueeze(2).broadcast_to([P, G, WC]), ALU.is_equal)\
                    .then_inc(hot_ready, 1)

            base_regs = [dve.alloc_register(f"base{j}") for j in range(G)]

            def load_bases(c):
                dve.load(base_regs, base_row[0:1, bass.ds(c, G)])
                return [dve.snap(r, min_val=0, max_val=(N - WINDOW) * NB) for r in base_regs]

            def add_window(buf, j, base):
                into = adj[:, :, bass.ds(base, WC)]
                dve.tensor_tensor(into, into, win[:, buf, j, 0:2 * WC].rearrange("p (a b) -> p a b", a=2),
                                  ALU.add).then_inc(added, 1)

            make_hot(0, slice(0, G))
            make_sel(0, slice(0, G))
            dve.wait_ge(zeros, 3)
            with dve.Fori(0, NG // 2 - 1) as t:
                for half in range(2):
                    dve.wait_ge(group_done, 2 * t + half + 1)
                    cols = bass.ds((2 * t + half + 1) * G, G)
                    make_hot(1 - half, cols)
                    make_sel(1 - half, cols)
                    bases = load_bases((2 * t + half) * G)
                    dve.wait_ge(group_done, 2 * t + half + 2)
                    for j in range(G):
                        dve.wait_ge(added, (2 * t + half) * G + j + 1)
                        add_window(half, j, bases[j])
            g = NG - 2
            dve.wait_ge(group_done, g + 1)
            make_hot(1, slice((NG - 1) * G, NG * G))
            make_sel(1, slice((NG - 1) * G, NG * G))
            for g in (NG - 2, NG - 1):
                bases = load_bases(g * G)
                dve.wait_ge(group_done, g + 2)
                for j in range(G):
                    dve.wait_ge(added, g * G + j + 1)
                    add_window(g % 2, j, bases[j])
            dve.wait_ge(added, CH + 1)

            uncovered = dve.value_load(flags[0:1, 0:1], min_val=0, max_val=1)
            with dve.If(uncovered > 0):
                dve.wait_ge(whigh_ready, NG)
                dve.wait_ge(wlow_ready, NG)
                gm = lambda ins, n: (ins.then_inc(gen_mask, 1), dve.wait_ge(gen_mask, n))
                gm(dve.tensor_scalar(tables[:, 0, :], tables[:, 0, :], float(WC), None, ALU.is_ge), 1)
                gm(dve.tensor_tensor(tables[:, 2, :], tables[:, 2, :], tables[:, 0, :], ALU.mult), 2)
                gm(dve.tensor_tensor(tables[:, 3, :], tables[:, 3, :], tables[:, 0, :], ALU.mult), 3)
                gm(dve.tensor_scalar(tables[:, 5, :], tables[:, 5, :], 1.0, None, ALU.add), 4)
                gm(dve.tensor_tensor(tables[:, 5, :], tables[:, 5, :], tables[:, 0, :], ALU.mult), 5)
                gm(dve.tensor_scalar(tables[:, 5, :], tables[:, 5, :], -1.0, float(P), ALU.add, ALU.mult), 6)
                gm(dve.tensor_tensor(tables[:, 5, :], tables[:, 5, :], tables[:, 1, :], ALU.add), 7)
                with dve.Fori(0, 2) as hf:
                    with dve.Fori(0, NB) as hb:
                        with dve.Fori(0, CH) as c:
                            n = (hf * NB + hb) * CH + c
                            col = bass.ds(c, 1)
                            gen_m = hot_flat[:, 0:3 * BANK]
                            dve.tensor_scalar(sel[:, 0, 0, :], ramp[:, 0:P], tables[:, 5, col], None,
                                              ALU.is_equal)
                            dve.tensor_scalar(gen_m[:, 0:BANK], ramp[:], tables[:, 4, col],
                                              tables[:, 2, col], ALU.is_equal, ALU.mult)
                            dve.tensor_scalar(gen_m[:, BANK:2 * BANK], ramp[:], tables[:, 4, col],
                                              tables[:, 3, col], ALU.is_equal, ALU.mult)
                            dve.tensor_scalar(gen_m[:, 2 * BANK:3 * BANK], ramp[:], tables[:, 4, col], None,
                                              ALU.is_equal).then_inc(gen_ready, 1)
                            dve.wait_ge(gen_done, n + 1)
                            for kind in range(2):
                                into = adj[:, kind, bass.ds(hf * BANK * NB + hb, BANK, step=NB)]
                                dve.tensor_tensor(into, into,
                                                  win[:, 0, 2 * kind:2 * kind + 2, :].rearrange("p a b -> p (a b)"),
                                                  ALU.add).then_inc(gen_added, 1)
                            dve.wait_ge(gen_added, 2 * n + 2)
                        dve.tensor_scalar(tables[:, 5, :], tables[:, 5, :], -float(P), None, ALU.add)\
                            .then_inc(gen_mask, 1)
                        dve.wait_ge(gen_mask, 8 + hf * (NB + 2) + hb)
                    dve.tensor_scalar(tables[:, 5, :], tables[:, 5, :], float(N), None, ALU.add)\
                        .then_inc(gen_mask, 1)
                    dve.tensor_scalar(tables[:, 4, :], tables[:, 4, :], -float(BANK), None, ALU.add)\
                        .then_inc(gen_mask, 1)
                    dve.wait_ge(gen_mask, 7 + (hf + 1) * (NB + 2))
            with dve.Else():
                dve.engine_nop()
            dve.sem_inc(adj_ready, 1)

            def step(ins):
                steps["norm"] += 1
                ins.then_inc(norm, 1)
                dve.wait_ge(norm, steps["norm"])
            step(dve.tensor_reduce(deg, adj[:, 0, :].rearrange("p (d h) -> p h d", h=NB), AX.X, ALU.add))
            step(dve.tensor_scalar(deg_pos, deg, 0.0, None, ALU.is_gt))
            dve.tensor_scalar(deg_safe, deg, 1.2e-38, None, ALU.max).then_inc(deg_ready, 1)
            dve.wait_ge(pow_ready, 1)
            dve.tensor_tensor(dinv, dinv, deg_pos, ALU.mult).then_inc(dinv_ready, 1)

            def tile_wait(name, i=0, more=0):
                dve.wait_ge(tile_done, index[(name, i)] + 1 + more)

            highs = [0]

            def lower(name, i, dest, high, scale=1.0, more=0):
                highs[0] += 1
                tile_wait(name, i, more)
                dve.wait_ge(high_ready, highs[0])
                tile = bank(name, i)
                if name == "at":
                    tile = tile.rearrange("p (b n) -> p b n", b=HALF)
                dve.scalar_tensor_tensor(out=dest, in0=shaped(tile, name), scalar=scale, in1=high.bitcast(F32),
                                         op0=ALU.mult, op1=ALU.subtract).then_inc(vector_freed, 1)

            for h in range(2):
                tile_wait("dinvb", h)
                dve.tensor_copy(col_scale[:, h * BANK:(h + 1) * BANK], bank("dinvb", h)).then_inc(vector_freed, 1)
            for n in range(2 * NB):
                j, h = divmod(n, 2)
                lower("at", n, at_low[:, j, h * BANK:(h + 1) * BANK].rearrange("p (b n) -> p b n", b=HALF),
                      at_high[:, h * HALF:(h + 1) * HALF, j, :], dinv[:, j:j + 1], more=1 - h)

            n_rows = [0]

            def row_scale(name, n):
                n_rows[0] += 1
                r = n_rows[0]
                tile_wait(name, n)
                if r > 3:
                    dve.wait_ge(row_low, r - 3)
                h = n // KD
                dve.tensor_tensor(tmp[:, (r - 1) % 3, :], bank(name, n), col_scale[:, h * BANK:(h + 1) * BANK],
                                  ALU.mult).then_inc(vector_freed, 1)
                return r

            def leak(r):
                row = tmp[:, (r - 1) % 3, :]
                dve.wait_ge(row_biased, r)
                dve.scalar_tensor_tensor(out=row, in0=row, scalar=SLOPE, in1=row, op0=ALU.mult,
                                         op1=ALU.max).then_inc(row_leaked, 1)

            tile_wait("y0", NB - 1)
            dve.wait_ge(split_low, split_count[("y0", NB - 1)])
            for n in range(2 * KD):
                leak(row_scale("h1", n))
                if n == 1:
                    dve.memset(ones_mat[:], 1.0).then_inc(ones_ready, 1)
                    dve.wait_ge(ones_ready, 1)
                    dve.tensor_reduce(cnt_sums[:], adj[:, 1, :].rearrange("p (d h) -> p d h", h=NB), AX.X,
                                      ALU.add).then_inc(sums_ready, 1)
            tile_wait("deg1")
            dve.tensor_scalar(deg1, bank("deg1")[:, 0:NB], 1.0, None, ALU.add).then_inc(vector_freed, 1)
            for b in range(NB):
                lower("y1", b, y_low[:, b, :], y_high[:, b, :])
            for h in range(2):
                tile_wait("disb", h)
                dve.tensor_copy(col_scale[:, h * BANK:(h + 1) * BANK], bank("disb", h)).then_inc(vector_freed, 1)
            read(dve, "disb", 1)
            step(dve.tensor_reduce(overflow, col_scale[:], AX.X, ALU.min))
            dve.tensor_scalar(flags[0:1, 1:2], overflow[0:1, :], EXACT_DEGREE ** -0.5, None, ALU.is_lt)\
                .then_inc(overflow_ready, 1)

            def layer_norm(b, z, dest, count):
                st, mv = stats[:, 6 * (b % 2):6 * (b % 2) + 6], mean_var[:, 2 * (b % 2):2 * (b % 2) + 2]
                r = rstd[:, 2 * (b % 2):2 * (b % 2) + 2]
                step(dve.bn_stats(st, z))
                step(dve.bn_aggr(mv, st))
                dve.tensor_scalar(r[:, 0:1], mv[:, 1:2], EPS, None, ALU.add).then_inc(var_ready, 1)
                dve.wait_ge(rstd_ready, count)
                return dve.tensor_scalar(dest, z, mv[:, 0:1], r[:, 1:2], ALU.subtract, ALU.mult)

            def scaled(b):
                return tmp[:, b % 3, :]

            def low_of(name, i):
                if name == "x1t":
                    lower(name, i, ht_low[:, :, i * P:(i + 1) * P], ht_high[:, :, i * P:(i + 1) * P])
                else:
                    lower(name, i, y_low[:, i, :], y_high[:, i, :], dis[:, i:i + 1])

            dve.wait_ge(row_low, 2 * KD)
            dve.wait_ge(x_again_in, 16)
            for b in range(NB):
                tile_wait("h2", b)
                z = scaled(b)
                dve.scalar_tensor_tensor(out=z, in0=bank("h2", b), scalar=dinv[:, b:b + 1],
                                         in1=bias_bc[:, 0, :], op0=ALU.mult, op1=ALU.add).then_inc(vector_freed, 1)
                read(dve, "h2", b)
                step(dve.scalar_tensor_tensor(out=z, in0=z, scalar=SLOPE, in1=z, op0=ALU.mult, op1=ALU.max))
                step(dve.tensor_tensor(z, z, xs[:, b, :], ALU.add))
                layer_norm(b, z, xs[:, b, :], b + 1).then_inc(x1_ready, 1)
                if b > 0:
                    low_of("x1t", b - 1)
            for i in range(NB):
                if i == NB - 1:
                    low_of("x1t", i)
                low_of("y2", i)
            for n in range(2 * KD):
                row_scale("h3", n)
            for i in range(NB):
                low_of("y3", i)
            dve.wait_ge(b2_in, 16)
            dve.wait_ge(row_low, 4 * KD)
            for b in range(NB):
                tile_wait("h4", b)
                z = scaled(b)
                dve.scalar_tensor_tensor(out=z, in0=bank("h4", b), scalar=dis[:, b:b + 1],
                                         in1=bias_bc[:, 1, :], op0=ALU.mult, op1=ALU.add).then_inc(vector_freed, 1)
                read(dve, "h4", b)
                step(dve.tensor_tensor(z, z, xs[:, b, :], ALU.add))
                layer_norm(b, z, xs[:, b, :], NB + b + 1).then_inc(out_ready, 1)


INPUTS = ["x", "src", "dst", "edge_weight", "L0_gnn_W_gcn", "L0_gnn_b_gcn", "L0_gnn_W_mlp", "L0_gnn_b_mlp",
          "L1_gnn_W1", "L1_gnn_b1", "L1_gnn_W2", "L1_gnn_b2"]


def kernel(**inputs):
    import numpy as np
    import concourse.bacc as bacc
    from concourse.bass_utils import run_bass_kernel_spmd

    nc = bacc.Bacc("TRN2", target_bir_lowering=False, num_devices=1)
    arrays, args = {}, []
    for name in INPUTS:
        a = np.ascontiguousarray(inputs[name])
        arrays[f"in_{name}"] = a
        args.append(nc.dram_tensor(f"in_{name}", a.shape, mybir.dt.from_np(a.dtype), kind="ExternalInput").ap())
    out = nc.dram_tensor("out", inputs["x"].shape, F32, kind="ExternalOutput").ap()
    gnn_resnorm(nc, *args, out)
    r = run_bass_kernel_spmd(nc, [arrays], core_ids=[0])
    return r.results[0]["out"]
```

```python
from contextlib import ExitStack

import concourse.bass as bass
from concourse import mybir

F32 = mybir.dt.float32
F32R = mybir.dt.float32r
I32 = mybir.dt.int32
ALU = mybir.AluOpType
ACT = mybir.ActivationFunctionType
AX = mybir.AxisListType

P = 128
BANK = 512
Y0_FIRST = 4
WINDOW = 12
BUFS = 3
G = 4
SLOPE = 0.01
EPS = 1e-5
PREP_TURN = 13
N_CONSTS = 4
FULL = False
EXACT_DEGREE = 4000.0


def gnn_resnorm(nc, x, src, dst, weight, wg, bg, wm, bm, w1, b1, w2, b2, out):
    N, D = x.shape
    E = src.shape[0]
    NB = N // P
    KD = D // P
    CH = E // P
    NG = CH // G
    WC = WINDOW * NB
    HALF = NB // 2
    assert D == BANK and CH == P and N * 1 == 2 * BANK and NB == 8 and KD == 4

    with ExitStack() as ctx:
        start = (nc.sbuf_base + 31) // 32 * 32
        KB = 1024
        ADJ, ATH, YR, HR, XR, WR, SM = (start + k * KB for k in (0, 64, 96, 128, 160, 176, 192))
        cursor = {}

        def at(name, region, shape, dtype):
            size = 4
            for n in shape[1:]:
                size *= n
            offset = cursor.get(region, region)
            cursor[region] = offset + (size + 31) // 32 * 32
            return nc.alloc_sbuf_tensor_at(name, shape, dtype, offset=offset)

        def again(region):
            cursor[region] = region

        adj = at("adj", ADJ, [P, 2, N * NB], F32)
        again(ADJ)
        at_low = at("at_low", ADJ, [P, NB, N], F32R)
        sel = at("sel", ATH, [P, BUFS, G, P], F32R)
        hot_row = (3 * BUFS * G + 1) * WC
        hot_all = at("hot", ATH, [P, hot_row], F32R)
        hot = hot_all[:, 0:3 * BUFS * G * WC].rearrange("p (b a g c) -> p b a g c", b=BUFS, a=3, g=G)
        ramp = at("ramp", ATH, [P, P], F32)
        tables = at("tables", ATH, [P, 6, P], F32)
        wg_raw = at("wg_raw", ATH, [P, KD, D], F32)
        gen_ramp = wg_raw[:, 0, :]
        assert cursor[ATH] <= YR
        again(ATH)
        at_high = at("at_high", ATH, [P, NB, NB, P], F32R)
        again(ATH)
        cnt = at("cnt", ATH, [P, NB, NB, P], F32R)
        wgt_high = at("wgt_high", YR, [P, KD, D], F32R)
        wgt_low = at("wgt_low", YR, [P, KD, D], F32R)
        wm_high = at("wm_high", YR, [P, KD, D], F32R)
        wm_raw = at("wm_raw", YR, [P, KD, D], F32)
        cursor[YR] -= 4 * KD * D
        wm_low = at("wm_low", YR, [P, KD, D], F32R)
        again(YR)
        y_high = at("y_high", YR, [P, NB, D], F32R)
        y_low = at("y_low", YR, [P, NB, D], F32R)
        ht_high = at("ht_high", HR, [P, KD, N], F32R)
        ht_low = at("ht_low", HR, [P, KD, N], F32R)
        x_first = at("x_first", XR, [P, NB, D], F32)
        again(XR)
        wcb_high = at("wcb_high", XR, [P, KD, D], F32R)
        wcb_low = at("wcb_low", XR, [P, KD, D], F32R)
        again(XR)
        xs = at("xs", XR, [P, NB, D], F32)
        wca_high = at("wca_high", WR, [P, KD, D], F32R)
        wca_low = at("wca_low", WR, [P, KD, D], F32R)
        again(WR)
        cnt_sums = at("cnt_sums", WR, [P, N], F32)
        ones_mat = at("ones_mat", WR, [P, 2], F32)
        again(WR)
        w12_high = at("w12_high", WR, [P, KD, D], F32R)
        w12_raw = at("w12_raw", WR, [P, KD, D], F32)
        cursor[WR] -= 4 * KD * D
        w12_low = at("w12_low", WR, [P, KD, D], F32R)
        tmp = at("tmp", SM, [P, 3, BANK], F32)
        again(SM)
        cursor[SM] += 2 * 4 * BANK
        bias_rows = at("bias_rows", SM, [3, D], F32)
        col_scale = at("col_scale", SM, [P, N], F32)
        bias_bc = at("bias_bc", SM, [P, 2, D], F32)
        ident = at("ident", SM, [P, P], F32)
        neg_ident = at("neg_ident", SM, [P, P], F32R)
        small = at("small", SM, [P, 104], F32)
        bg_raw = at("bg_raw", SM, [P, KD], F32)
        bg_parts = at("bg_parts", SM, [P, KD, 2], F32R)
        flags = at("flags", SM, [1, 8], I32)
        assert cursor[SM] <= nc.sbuf_usable_end, (cursor[SM], nc.sbuf_usable_end)
        EDGE = start + 192 * KB + 4 * 3 * BANK
        src_i = at("src_i", EDGE, [P, P], I32)
        dst_i = at("dst_i", EDGE, [P, P], I32)
        w_e = at("w_e", EDGE, [P, P], F32)
        dst_f = at("dst_f", EDGE, [P, P], F32)
        hi_i = at("hi_i", EDGE, [P, P], I32)
        lo_i = at("lo_i", EDGE, [P, P], I32)
        hi_f = at("hi_f", EDGE, [P, P], F32)
        lo_f = at("lo_f", EDGE, [P, P], F32)
        col_f = at("col_f", EDGE, [P, P], F32)
        w_high = at("w_high", EDGE, [P, P], F32R)
        w_low = at("w_low", EDGE, [P, P], F32)
        ones3 = at("ones3", EDGE, [3, P], F32)
        base_row = at("base_row", EDGE, [1, P], I32)
        assert cursor[EDGE] <= EDGE + 8 * KB

        deg = small[:, 0:8]
        dinv = small[:, 8:16]
        dis = small[:, 16:24]
        power = small[:, 24:32]
        deg_pos = small[:, 32:40]
        deg_safe = small[:, 40:48]
        base_max = small[:, 48:50]
        pidx = small[:, 50:51]
        bias_t = small[:, 52:56]
        b1_t = small[:, 56:60]
        stats = small[:, 60:72]
        mean_var = small[:, 72:76]
        rstd = small[:, 76:80]
        overflow = small[:, 80:81]
        deg1 = small[:, 84:92]
        max_col = small[0:1, 100:101]

        win = ctx.enter_context(nc.psum_tensor("win", [P, 2, G, 256], F32))
        work = ctx.enter_context(nc.psum_tensor("work", [P, 4, BANK], F32))
        WB = 4

        SCALAR, VECTOR, REST = "scalar", "vector", "rest"
        tiles = [("tab", 0, VECTOR), ("tab", 1, VECTOR)]
        first_fill = len(tiles)
        wgt = [[(f"wgt{l}", k, SCALAR) for k in range(KD)] for l in (0, 1)]
        wc = [[(f"wc{l}", k, REST) for k in range(KD)] for l in (0, 1)]
        xt = [("xt", b, SCALAR) for b in range(NB)]
        bias, biasb = [[(f"{b}{l}", 0, SCALAR) for l in (0, 1)] for b in ("bias", "biasb")]
        table = {0: [wgt[0][0]], 1: [wgt[0][1]], 2: [wgt[0][2]], 3: [wgt[0][3]],
                 8: [xt[0]], 9: [bias[0]], 10: [xt[1]], 11: [wc[0][0]], 12: [xt[2]], 13: [wc[0][1]], 14: [xt[3]],
                 15: [wc[0][2]], 16: [xt[4]], 17: [wc[0][3]],
                 18: [wgt[1][0]], 19: [wgt[1][1]], 20: [wgt[1][2]], 21: [wgt[1][3]],
                 24: [biasb[0], xt[5]], 25: [xt[6]], 26: [xt[7]], 27: [bias[1]], 29: [wc[1][0]], 30: [biasb[1]],
                 31: [wc[1][1]]}
        slots = [table.get(n, []) for n in range(NG)]
        wm_slots = {3 + k: (0, k) for k in range(KD)} | {5 * KD + k: (1, k) for k in range(KD)}
        tiles += [t for slot in slots for t in slot]
        slot = lambda n: slots[n] if 0 <= n < NG else []
        fills = tiles[first_fill:]
        late_rest = [t for t in slots[NG - 2] + slots[NG - 1] if t[2] == REST]
        mixed = wc[1][2:] + [("y0", b, REST) for b in range(Y0_FIRST)]
        for j in range(NB):
            mixed += [("at", 2 * j, VECTOR), ("at", 2 * j + 1, VECTOR)]
            if Y0_FIRST + j < NB:
                mixed += [("y0", Y0_FIRST + j, REST)]
        mixed += [("dinvb", h, VECTOR) for h in range(2)]
        tiles += mixed
        tiles += [("h1", f, VECTOR) for f in range(2 * KD)]
        tiles += [("deg1", 0, VECTOR)]
        tiles += [("y1", b, VECTOR) for b in range(NB)]
        tiles += [("disb", h, VECTOR) for h in range(2)]
        tiles += [("h2", 0, VECTOR)]
        for b in range(1, NB):
            tiles += [("h2", b, VECTOR), ("x1t", b - 1, VECTOR)]
        tiles += [("y2", b, VECTOR) for b in range(NB - 1)] + [("x1t", NB - 1, VECTOR)]
        tiles += [("y2", NB - 1, VECTOR)]
        tiles += [("h3", f, VECTOR) for f in range(2 * KD)]
        tiles += [("y3", b, VECTOR) for b in range(NB)]
        tiles += [("h4", b, VECTOR) for b in range(NB)]
        index = {t[:2]: n for n, t in enumerate(tiles)}
        done_at, freed = {}, {SCALAR: 0, VECTOR: 0, REST: 0}
        for n, t in enumerate(tiles):
            freed[t[2]] += 1
            done_at[n] = (t[2], freed[t[2]])

        def read(eng, name, i=0):
            who, value = done_at[index[(name, i)]]
            eng.wait_ge({SCALAR: scalar_freed, VECTOR: vector_freed, REST: rest_freed}[who], value)

        def bank(name, i=0):
            return work[:, index[(name, i)] % WB, :]

        sem = lambda name: ctx.enter_context(nc.semaphore(name))
        edges_in = sem("edges_in")
        x_in, x_again_in = sem("x_in"), sem("x_again_in")
        wg_in, wm_in = sem("wg_in"), sem("wm_in")
        bg_in, bm_in = sem("bg_in"), sem("bm_in")
        b1_in, b2_in = sem("b1_in"), sem("b2_in")
        w1_in, w2_in = sem("w1_in"), sem("w2_in")
        consts = sem("consts")
        zeros = sem("zeros")
        prep = sem("prep")
        tile_done = sem("tile_done")
        scalar_freed = sem("scalar_freed")
        neg_ready = sem("neg_ready")
        rest_freed = sem("rest_freed")
        rest_high = sem("rest_high")
        rest_done = sem("rest_done")
        vector_freed = sem("vector_freed")
        sel_ready = sem("sel_ready")
        hot_ready = sem("hot_ready")
        whigh_ready = sem("whigh_ready")
        wlow_ready = sem("wlow_ready")
        group_done = sem("group_done")
        added = sem("added")
        adj_ready = sem("adj_ready")
        gen_ready, gen_done, gen_added = sem("gen_ready"), sem("gen_done"), sem("gen_added")
        gen_mask = sem("gen_mask")
        split_copy = sem("split_copy")
        split_low = sem("split_low")
        wm_split_high, wm_split_low = sem("wm_split_high"), sem("wm_split_low")
        bg_high, bg_split = sem("bg_high"), sem("bg_split")
        deg_ready = sem("deg_ready")
        pow_ready = sem("pow_ready")
        dinv_ready = sem("dinv_ready")
        high_ready = sem("high_ready")
        sums_ready = sem("sums_ready")
        ones_ready = sem("ones_ready")
        row_biased, row_leaked = sem("row_biased"), sem("row_leaked")
        row_high, row_low = sem("row_high"), sem("row_low")
        norm = sem("norm")
        var_ready, rstd_ready = sem("var_ready"), sem("rstd_ready")
        x1_ready = sem("x1_ready")
        cnt_ready = sem("cnt_ready")
        overflow_ready = sem("overflow_ready")
        w1_high, w1_low, w2_high, w2_low = sem("w1_high"), sem("w1_low"), sem("w2_high"), sem("w2_low")
        out_ready, stored = sem("out_ready"), sem("stored")

        split_count, rest_count = {}, {}
        for t in fills + mixed:
            if t[2] == SCALAR and not t[0].startswith("bias"):
                split_count[t[:2]] = len(split_count) + 1
            if t[2] == REST:
                rest_count[t[:2]] = len(rest_count) + 1

        def parts_of(t):
            name, i = t[0], t[1]
            if name.startswith("wgt"):
                return wgt_high[:, i, :], wgt_low[:, i, :]
            if name == "xt":
                return (ht_high[:, :, i * P:(i + 1) * P], ht_low[:, :, i * P:(i + 1) * P])
            if name == "wc0":
                return wca_high[:, i, :], wca_low[:, i, :]
            if name == "wc1":
                return wcb_high[:, i, :], wcb_low[:, i, :]
            return y_high[:, i, :], y_low[:, i, :]

        def shaped(ap, name):
            return ap.rearrange("p (k n) -> p k n", k=KD) if name in ("xt", "x1t") else ap

        block = ctx.enter_context(nc.Block())

        @block.sync
        def _(sp):
            rows = "(c e) -> c e"
            sp.dma_start(dst_i[:], dst.rearrange(rows, e=P)).then_inc(edges_in, 16)
            sp.dma_start(src_i[:], src.rearrange(rows, e=P)).then_inc(edges_in, 16)
            sp.dma_start(w_e[:], weight.rearrange(rows, e=P)).then_inc(edges_in, 16)
            by_k = "(k p) n -> p k n"
            sp.dma_start(wg_raw[:], wg[0].rearrange(by_k, p=P)).then_inc(wg_in, 16)
            sp.dma_start(wm_raw[:], wm[0].rearrange(by_k, p=P)).then_inc(wm_in, 16)
            sp.dma_start(x_first[:], x.rearrange(by_k, p=P)).then_inc(x_in, 16)
            with nc.allow_non_contiguous_dma(reason="bias columns"):
                sp.dma_start(bg_raw[:], bg[0].rearrange("(k p) -> p k", p=P)).then_inc(bg_in, 16)
                sp.dma_start(b1_t, b1.rearrange("(k p) -> p k", p=P)).then_inc(b1_in, 16)
            sp.dma_start(bias_rows[2:3, :], bm[0:1, :]).then_inc(bm_in, 16)
            sp.wait_ge(tile_done, index[("wgt0", KD - 1)] + 1)
            sp.dma_start(wg_raw[:], wg[1].rearrange(by_k, p=P)).then_inc(wg_in, 16)
            sp.wait_ge(bg_split, 1)
            with nc.allow_non_contiguous_dma(reason="bias columns"):
                sp.dma_start(bg_raw[:], bg[1].rearrange("(k p) -> p k", p=P)).then_inc(bg_in, 16)
            sp.wait_ge(tile_done, index[("wc0", KD - 1)] + 1)
            sp.dma_start(wm_raw[:], wm[1].rearrange(by_k, p=P)).then_inc(wm_in, 16)
            sp.wait_ge(tile_done, index[("biasb0", 0)] + 1)
            sp.dma_start(bias_rows[2:3, :], bm[1:2, :]).then_inc(bm_in, 16)
            sp.wait_ge(tile_done, index[("biasb1", 0)] + 1)
            sp.wait_ge(adj_ready, 1)
            sp.dma_start(bias_bc[:, 1, :], b2.rearrange("(a n) -> a n", a=1).broadcast_to([P, D])).then_inc(b2_in, 16)
            sp.wait_ge(tile_done, index[("deg1", 0)] + 1)
            sp.dma_start(w12_raw[:], w1.rearrange(by_k, p=P)).then_inc(w1_in, 16)
            sp.wait_ge(tile_done, index[("y1", NB - 1)] + 1)
            sp.dma_start(xs[:], x.rearrange(by_k, p=P)).then_inc(x_again_in, 16)
            sp.wait_ge(tile_done, index[("y2", NB - 1)] + 1)
            sp.dma_start(w12_raw[:], w2.rearrange(by_k, p=P)).then_inc(w2_in, 16)
            for b in range(NB):
                sp.wait_ge(out_ready, b + 1)
                sp.dma_start(out[b * P:(b + 1) * P, :], xs[:, b, :]).then_inc(stored, 16)
            sp.wait_ge(stored, 16 * NB)

        @block.gpsimd
        def _(pool):
            pool.iota(ramp[:], [[1, P]], base=0, channel_multiplier=0,
                      allow_small_or_imprecise_dtypes=True).then_inc(consts, 1)
            pool.iota(pidx, [[0, 1]], base=0, channel_multiplier=1,
                      allow_small_or_imprecise_dtypes=True).then_inc(consts, 1)
            pool.memset(power, -0.5).then_inc(consts, 1)
            pool.memset(ones3[:], 1.0).then_inc(consts, 1)
            pool.memset(hot_all[:, 3 * BUFS * G * WC:].bitcast(F32), 0.0).then_inc(zeros, 1)
            pool.memset(adj[:, 1, :], 0.0).then_inc(zeros, 1)

            def weigh(g):
                pool.wait_ge(hot_ready, 2 * g + 2)
                w = tables[:, 2, g * G:(g + 1) * G].unsqueeze(2).broadcast_to([P, G, WC])
                pool.tensor_tensor(hot[:, g % BUFS, 0], hot[:, g % BUFS, 1].bitcast(F32), w,
                                   ALU.mult).then_inc(whigh_ready, 1)

            def low(t):
                n = split_count[t[:2]]
                read(pool, *t[:2])
                hi, lo = parts_of(t)
                pool.tensor_tensor(lo, shaped(tmp[:, n % 2, :], t[0]), hi.bitcast(F32),
                                   ALU.subtract).then_inc(split_low, 1)

            def to_power(safe, res, count):
                pool.tensor_tensor(res, safe, power[:, 0:count], ALU.pow).then_inc(pow_ready, 1)

            def bg_split_up(l):
                pool.wait_ge(bg_in, 16 * (l + 1))
                if l == 1:
                    pool.wait_ge(tile_done, index[("bias0", 0)] + 1)
                pool.tensor_copy(bg_parts[:, :, 0], bg_raw[:]).then_inc(bg_high, 1)
                pool.wait_ge(bg_high, l + 1)
                pool.tensor_tensor(bg_parts[:, :, 1], bg_raw[:], bg_parts[:, :, 0].bitcast(F32),
                                   ALU.subtract).then_inc(bg_split, 1)

            def wm_lower(l, k):
                pool.wait_ge(wm_split_high, KD * l + k + 1)
                pool.tensor_tensor(wm_low[:, k, :], wm_raw[:, k, :], wm_high[:, k, :].bitcast(F32),
                                   ALU.subtract).then_inc(wm_split_low, 1)

            pool.wait_ge(vector_freed, 2)
            weigh(0)
            weigh(1)
            for n in range(NG + 1):
                if n + 2 < NG:
                    weigh(n + 2)
                for t in slot(n - 1):
                    if t[:2] in split_count:
                        low(t)
                if n - 1 in wm_slots:
                    l, k = wm_slots[n - 1]
                    wm_lower(l, k)
                    if k == 0:
                        bg_split_up(l)
            pool.wait_ge(deg_ready, 1)
            to_power(deg_safe, dinv, NB)
            n_rows = [0]

            def row_lower(dest, high):
                n_rows[0] += 1
                n = n_rows[0]
                pool.wait_ge(row_high, n)
                pool.tensor_tensor(dest, tmp[:, (n - 1) % 3, :], high.bitcast(F32),
                                   ALU.subtract).then_inc(row_low, 1)

            def w_lower(ready, high_sem):
                pool.wait_ge(high_sem, 1)
                pool.tensor_tensor(w12_low[:], w12_raw[:], w12_high[:].bitcast(F32),
                                   ALU.subtract).then_inc(ready, 1)

            for n in range(2 * KD):
                h, f = divmod(n, KD)
                row_lower(ht_low[:, f, h * BANK:(h + 1) * BANK], ht_high[:, f, h * BANK:(h + 1) * BANK])
            read(pool, "deg1")
            to_power(deg1, dis, NB)
            w_lower(w1_low, w1_high)
            for b in range(NB):
                pool.wait_ge(var_ready, b + 1)
                r = rstd[:, 2 * (b % 2):2 * (b % 2) + 2]
                pool.tensor_tensor(r[:, 1:2], r[:, 0:1], power[:, 0:1], ALU.pow).then_inc(rstd_ready, 1)
                pool.wait_ge(tile_done, index[("h2", b)] + 1)
                block_of = adj[:, 1, b * P * NB:(b + 1) * P * NB].rearrange("p (d h) -> p h d", h=NB)
                if b > 0:
                    pool.tensor_copy(cnt[:, b, 0:b, :], block_of[:, 0:b, :]).then_inc(cnt_ready, 1)
                if b < NB - 1:
                    pool.tensor_copy(cnt[:, b, b + 1:NB, :], block_of[:, b + 1:NB, :]).then_inc(cnt_ready, 1)
                pool.tensor_tensor(cnt[:, b, b, :], block_of[:, b, :], ident[:], ALU.add).then_inc(cnt_ready, 1)
            for n in range(2 * KD):
                h, f = divmod(n, KD)
                row_lower(ht_low[:, f, h * BANK:(h + 1) * BANK], ht_high[:, f, h * BANK:(h + 1) * BANK])
                if n == 2:
                    w_lower(w2_low, w2_high)
            for b in range(NB):
                pool.wait_ge(var_ready, NB + b + 1)
                r = rstd[:, 2 * (b % 2):2 * (b % 2) + 2]
                pool.tensor_tensor(r[:, 1:2], r[:, 0:1], power[:, 0:1], ALU.pow).then_inc(rstd_ready, 1)

        @block.scalar
        def _(act):
            def weigh_low(g):
                act.wait_ge(hot_ready, 2 * g + 2)
                for j in range(G):
                    c = g * G + j
                    ins = act.activation(hot[:, g % BUFS, 2, j, :], hot[:, g % BUFS, 1, j, :].bitcast(F32), ACT.Copy,
                                         scale=tables[:, 3, c:c + 1])
                ins.then_inc(wlow_ready, 1)

            def wm_upper(l, k):
                act.wait_ge(wm_in, 16 * (l + 1))
                act.activation(wm_high[:, k, :], wm_raw[:, k, :], ACT.Copy).then_inc(wm_split_high, 1)

            def fill(t):
                name, i = t[0], t[1]
                act.wait_ge(tile_done, index[(name, i)] + 1)
                if name.startswith("bias"):
                    l = int(name[-1])
                    if not name.startswith("biasb"):
                        act.activation(bias_rows[0:2, :], bank(name)[0:2, :], ACT.Copy).then_inc(scalar_freed, 1)
                    elif l == 0:
                        act.activation(bias_t, bank(name)[:, 0:KD], ACT.Copy).then_inc(scalar_freed, 1)
                    else:
                        act.activation(bias_bc[:, 0, :], bank(name), ACT.Copy).then_inc(scalar_freed, 1)
                    return
                hi, lo = parts_of(t)
                if t[:2] in rest_count:
                    if name.startswith("y0") and i == 0:
                        act.wait_ge(wm_split_low, 2 * KD)
                    act.activation(hi, bank(name, i), ACT.Copy).then_inc(rest_high, 1)
                    return
                n = split_count[t[:2]]
                if n > 2:
                    act.wait_ge(split_low, n - 2)
                act.activation(tmp[:, n % 2, :], bank(name, i), ACT.Copy).then_inc(split_copy, 1)
                act.activation(hi, shaped(bank(name, i), name), ACT.Copy).then_inc(scalar_freed, 1)

            def rest(t):
                act.wait_ge(rest_done, rest_count[t[:2]])
                act.activation(parts_of(t)[1], bank(*t[:2]), ACT.Copy).then_inc(rest_freed, 1)

            act.wait_ge(consts, N_CONSTS)
            act.activation(adj[:, 0, :].rearrange("p (a b) -> p a b", b=P),
                           ramp[:].unsqueeze(1).broadcast_to([P, N * NB // P, P]), ACT.Copy, scale=0.0)\
                .then_inc(zeros, 1)
            act.wait_ge(vector_freed, 2)
            weigh_low(0)
            weigh_low(1)
            for n in range(NG + 1):
                if n + 2 < NG:
                    weigh_low(n + 2)
                for t in slot(n - 2) if n < NG else []:
                    if t[:2] in rest_count:
                        rest(t)
                for t in slot(n - 1):
                    fill(t)
                if n - 1 in wm_slots:
                    wm_upper(*wm_slots[n - 1])

            def upper(name, i, dest, scale=None):
                act.wait_ge(tile_done, index[(name, i)] + 1)
                kw = {} if scale is None else {"scale": scale}
                tile = bank(name, i)
                if name == "at":
                    tile = tile.rearrange("p (b n) -> p b n", b=HALF)
                act.activation(dest, shaped(tile, name), ACT.Copy, **kw).then_inc(high_ready, 1)

            for t in late_rest:
                rest(t)
            for n, t in enumerate(mixed):
                if t[2] == REST:
                    fill(t)
                if n > 0 and mixed[n - 1][2] == REST:
                    rest(mixed[n - 1])
                if t[0] == "at":
                    j, h = divmod(t[1], 2)
                    if t[1] == 0:
                        act.wait_ge(dinv_ready, 1)
                    upper("at", t[1], at_high[:, h * HALF:(h + 1) * HALF, j, :], dinv[:, j:j + 1])

            n_rows = [0]

            def row_steps(bias, f, h, leaky):
                n_rows[0] += 1
                n = n_rows[0]
                row = tmp[:, (n - 1) % 3, :]
                read(act, "h1" if leaky else "h3", h * KD + f)
                act.activation(row, row, ACT.Identity if leaky else ACT.Relu, bias=bias[:, f:f + 1])\
                    .then_inc(row_biased, 1)
                if leaky:
                    act.wait_ge(row_leaked, n)
                else:
                    act.wait_ge(row_biased, n)
                act.activation(ht_high[:, f, h * BANK:(h + 1) * BANK], row, ACT.Copy).then_inc(row_high, 1)

            for n in range(2 * KD):
                h, f = divmod(n, KD)
                row_steps(bias_t, f, h, True)
            for b in range(NB):
                upper("y1", b, y_high[:, b, :])
            act.wait_ge(w1_in, 16)
            act.activation(w12_high[:], w12_raw[:], ACT.Copy).then_inc(w1_high, 1)
            for name, i, _ in tiles[index[("x1t", 0)]:index[("y2", NB - 1)] + 1]:
                if name == "x1t":
                    upper(name, i, ht_high[:, :, i * P:(i + 1) * P])
                elif name == "y2":
                    upper(name, i, y_high[:, i, :], dis[:, i:i + 1])
            for n in range(2 * KD):
                h, f = divmod(n, KD)
                row_steps(b1_t, f, h, False)
                if n == 2:
                    act.wait_ge(w2_in, 16)
                    act.activation(w12_high[:], w12_raw[:], ACT.Copy).then_inc(w2_high, 1)
            for b in range(NB):
                upper("y3", b, y_high[:, b, :], dis[:, b:b + 1])

        @block.tensor
        def _(pe):
            state = {"n": 0}

            def begin(name, i=0):
                n = index[(name, i)]
                assert n == state["n"], (name, i, n, state["n"])
                state["n"] += 1
                if n >= WB:
                    read(pe, *tiles[n - WB][:2])
                return work[:, n % WB, :]

            def split_product(dest, stationary, moving, wait=None):
                last = len(stationary) - 1
                for k, ((sh, sl), (mh, ml)) in enumerate(zip(stationary, moving)):
                    if wait is not None:
                        wait(k)
                    pairs = [(sh, mh)]
                    if sl is not None:
                        pairs += [(sl, mh)]
                    if ml is not None:
                        pairs += [(sh, ml)]
                    for n, (s, m) in enumerate(pairs):
                        ins = pe.matmul(dest, s, m, start=(k == 0 and n == 0),
                                        stop=(k == last and n == len(pairs) - 1))
                return ins

            def turn(dest, blocks):
                for n, b in enumerate(blocks):
                    ins = pe.transpose(dest[:, n * P:(n + 1) * P], b, ident[:])
                return ins

            def group(g):
                pe.wait_ge(sel_ready, 2 * g + 2)
                pe.wait_ge(whigh_ready, g + 1)
                pe.wait_ge(wlow_ready, g + 1)
                if g >= 2:
                    pe.wait_ge(added, G * (g - 1))
                b = g % BUFS
                for j in range(G):
                    into = win[:, g % 2, j, 0:2 * WC]
                    pe.matmul(into, sel[:, b, j, :], hot[:, b, 0:2, j, :], start=True, stop=False)
                    low_at = ((3 * b + 2) * G + j) * WC
                    zero_at = 3 * BUFS * G * WC
                    low_zero = bass.AP(tensor=hot_all, offset=low_at,
                                       ap=[[hot_row, P], [zero_at - low_at, 2], [1, WC]])
                    ins = pe.matmul(into, sel[:, b, j, :], low_zero, start=False, stop=True)
                ins.then_inc(group_done, 1)

            def kblocks(high, low, f=None):
                cut = (lambda a, k: a[:, k, f * P:(f + 1) * P]) if f is not None else (lambda a, k: a[:, k, :])
                return [(cut(high, k), cut(low, k)) for k in range(KD)]

            def product(t, half):
                name, i = t[0], t[1]
                l = int(name[-1])
                if i == 0 and half == 0:
                    pe.wait_ge(wm_split_low, KD * (l + 1))
                    pe.wait_ge(split_low, split_count[(f"wgt{l}", KD - 1)])
                b = begin(name, i) if half == 0 else bank(name, i)
                for k in (0, 1) if half == 0 else (2, 3):
                    s = slice(i * P, (i + 1) * P)
                    pe.matmul(b, wgt_high[:, k, s], wm_high[:, k, :], start=(k == 0), stop=False)
                    pe.matmul(b, wgt_low[:, k, s], wm_high[:, k, :], start=False, stop=False)
                    ins = pe.matmul(b, wgt_high[:, k, s], wm_low[:, k, :], start=False, stop=(k == KD - 1))
                if half == 1:
                    ins.then_inc(tile_done, 1)

            def filler(t):
                name, i = t[0], t[1]
                if name.startswith("wc"):
                    return product(t, 1)
                b = begin(name, i)
                if name.startswith("wgt"):
                    l = int(name[-1])
                    if i == 0:
                        pe.wait_ge(wg_in, 16 * (l + 1))
                    ins = turn(b, [wg_raw[:, m, i * P:(i + 1) * P] for m in range(KD)])
                elif name == "xt":
                    if i == 0:
                        pe.wait_ge(x_in, 16)
                    ins = turn(b, [x_first[:, i, k * P:(k + 1) * P] for k in range(KD)])
                elif name.startswith("biasb"):
                    l = int(name[-1])
                    pe.wait_ge(bm_in, 16 * (l + 1))
                    read(pe, f"bias{l}")
                    if l == 0:
                        for f in range(KD):
                            ins = pe.matmul(b[:, f:f + 1], bias_rows[:, f * P:(f + 1) * P], ones3[:, 0:1],
                                            start=True, stop=True)
                    else:
                        ins = pe.matmul(b, ones3[:], bias_rows[:], start=True, stop=True)
                else:
                    l = int(name[-1])
                    pe.wait_ge(bg_split, l + 1)
                    pe.wait_ge(wm_split_low, KD * (l + 1))
                    ops = [(bg_parts[:, k, :], m[:, k, :]) for k in range(KD) for m in (wm_high, wm_low)]
                    for n, (s, m) in enumerate(ops):
                        ins = pe.matmul(b[0:2, :], s, m, start=(n == 0), stop=(n == len(ops) - 1))
                ins.then_inc(tile_done, 1)

            pe.wait_ge(consts, N_CONSTS)
            pe.wait_ge(prep, PREP_TURN)
            pe.wait_ge(neg_ready, 1)
            b = begin("tab", 0)
            turn(b, [col_f[:]]).then_inc(group_done, 1)
            turn(b[:, P:], [lo_f[:], w_high[:].bitcast(F32), w_low[:]]).then_inc(tile_done, 1)
            b = begin("tab", 1)
            turn(b, [dst_f[:], hi_f[:]])
            for n in range(2):
                ins = pe.transpose(b[0:1, (2 + n) * P:(3 + n) * P], base_max[:, n:n + 1], ident[:])
            ins.then_inc(tile_done, 1)

            def subtract_high(t):
                pe.wait_ge(rest_high, rest_count[t[:2]])
                pe.matmul(bank(*t[:2]), neg_ident[:], parts_of(t)[0], start=False, stop=True,
                          skip_group_check=True).then_inc(rest_done, 1)

            for n in range(NG):
                group(n)
                for t in slot(n - 2):
                    if t[:2] in rest_count:
                        subtract_high(t)
                for t in slot(n):
                    filler(t)
                for t in slot(n + 1):
                    if t[0].startswith("wc"):
                        product(t, 0)
            for t in late_rest:
                subtract_high(t)

            uncovered = pe.value_load(flags[0:1, 0:1], min_val=0, max_val=1)
            gen_m = hot_all[:, 0:3 * BANK]
            with pe.If(uncovered > 0):
                with pe.Fori(0, 2 * NB) as t:
                    with pe.Fori(0, CH) as c:
                        pe.wait_ge(gen_ready, t * CH + c + 1)
                        first = win[:, 0, 0:2, :].rearrange("p a b -> p (a b)")
                        second = win[:, 0, 2:4, :].rearrange("p a b -> p (a b)")
                        pe.matmul(first, sel[:, 0, 0, :], gen_m[:, 0:BANK], start=True, stop=False)
                        pe.matmul(first, sel[:, 0, 0, :], gen_m[:, BANK:2 * BANK], start=False, stop=True)
                        pe.matmul(second, sel[:, 0, 0, :], gen_m[:, 2 * BANK:3 * BANK], start=True, stop=True)\
                            .then_inc(gen_done, 1)
            with pe.Else():
                pe.nop()

            def y_tile(name, i, high, low, wait=None):
                return split_product(begin(name, i),
                                     [(ht_high[:, k, i * P:(i + 1) * P], ht_low[:, k, i * P:(i + 1) * P])
                                      for k in range(KD)],
                                     kblocks(high, low), wait)

            pe.wait_ge(split_low, split_count[("xt", NB - 1)])
            read(pe, "wc0", KD - 1)
            def spread(name, h, scales):
                b = begin(name, h)
                for n in range(HALF):
                    hb = h * HALF + n
                    ins = pe.matmul(b[:, n * P:(n + 1) * P], scales[:, hb:hb + 1].broadcast_to([P, P]), ident[:],
                                    start=True, stop=True)
                ins.then_inc(tile_done, 1)

            for n, (name, i, _) in enumerate(mixed):
                if name == "wc1":
                    product((name, i), 0)
                    product((name, i), 1)
                elif name == "y0":
                    y_tile("y0", i, wca_high, wca_low).then_inc(tile_done, 1)
                elif name == "at":
                    j, h = divmod(i, 2)
                    if i == 0:
                        pe.wait_ge(adj_ready, 1)
                    turn(begin("at", i), [adj[:, 0, j * P * NB + hb:(j + 1) * P * NB:NB]
                                          for hb in range(h * HALF, (h + 1) * HALF)]).then_inc(tile_done, 1)
                else:
                    if i == 0:
                        pe.wait_ge(dinv_ready, 1)
                    spread("dinvb", i, dinv)
                if n > 0 and mixed[n - 1][2] == REST:
                    subtract_high(mixed[n - 1])

            read(pe, "y0", NB - 1)
            for n in range(2 * KD):
                h, f = divmod(n, KD)
                split_product(begin("h1", n),
                              [(y_high[:, j, f * P:(f + 1) * P], y_low[:, j, f * P:(f + 1) * P])
                               for j in range(NB)],
                              [(at_high[:, h * HALF:(h + 1) * HALF, j, :], at_low[:, j, h * BANK:(h + 1) * BANK])
                               for j in range(NB)],
                              lambda j: read(pe, "at", 2 * j + 1) if n == 0 else None).then_inc(tile_done, 1)
            pe.wait_ge(sums_ready, 1)
            b = begin("deg1")
            for n in range(NB):
                ins = pe.matmul(b[:, n:n + 1], cnt_sums[:, n * P:(n + 1) * P], ones_mat[:, 0:1],
                                start=True, stop=True)
            ins.then_inc(tile_done, 1)
            for i in range(NB):
                y_tile("y1", i, wcb_high, wcb_low,
                       lambda k: pe.wait_ge(row_low, KD * (i // HALF) + k + 1) if i % HALF == 0 else None)\
                    .then_inc(tile_done, 1)
            pe.wait_ge(pow_ready, 2)
            for h in range(2):
                spread("disb", h, dis)
            def x1_turn(i):
                pe.wait_ge(x1_ready, i + 1)
                turn(begin("x1t", i), [xs[:, i, k * P:(k + 1) * P] for k in range(KD)]).then_inc(tile_done, 1)

            for i in range(NB):
                split_product(begin("h2", i),
                              [(at_high[:, i, j, :], at_low[:, j, i * P:(i + 1) * P]) for j in range(NB)],
                              [(y_high[:, j, :], y_low[:, j, :]) for j in range(NB)],
                              lambda j: read(pe, "y1", j) if i == 0 else None).then_inc(tile_done, 1)
                if i > 0:
                    x1_turn(i - 1)
            pe.wait_ge(w1_low, 1)
            for i in range(NB):
                if i == NB - 1:
                    x1_turn(i)
                read(pe, "x1t", i)
                y_tile("y2", i, w12_high, w12_low).then_inc(tile_done, 1)
            pe.wait_ge(overflow_ready, 1)
            over = pe.value_load(flags[0:1, 1:2], min_val=0, max_val=1)
            pe.wait_ge(cnt_ready, 3 * NB - 2)

            def counts_of(hb, d0, d1):
                return adj[:, 1, d0 * NB + hb:d1 * NB:NB]

            def h3(full):
                for n in range(2 * KD):
                    h, f = divmod(n, KD)
                    b = begin("h3", n) if not full else again_tile("h3", n)
                    s = [(y_high[:, j, f * P:(f + 1) * P], y_low[:, j, f * P:(f + 1) * P]) for j in range(NB)]
                    if not full:
                        split_product(b, s, [(cnt[:, h * HALF:(h + 1) * HALF, j, :], None) for j in range(NB)],
                                      lambda j: read(pe, "y2", j) if n == 0 else None).then_inc(tile_done, 1)
                        continue
                    read(pe, "y2", NB - 1)
                    ops = []
                    for j in range(NB):
                        for y in s[j]:
                            ops.append((b, y.bitcast(F32), counts_of(j, h * BANK, (h + 1) * BANK)))
                            if j // HALF == h:
                                c = (j % HALF) * P
                                ops.append((b[:, c:c + P], y.bitcast(F32), ident[:]))
                    for m, (d, s_, mv) in enumerate(ops):
                        ins = pe.matmul(d, s_, mv, start=(m == 0), stop=(m == len(ops) - 1),
                                        skip_group_check=True)
                    ins.then_inc(tile_done, 1)

            def h4(full):
                for i in range(NB):
                    b = begin("h4", i) if not full else again_tile("h4", i)
                    if not full:
                        split_product(b, [(cnt[:, i, j, :], None) for j in range(NB)],
                                      [(y_high[:, j, :], y_low[:, j, :]) for j in range(NB)],
                                      lambda j: read(pe, "y3", j) if i == 0 else None).then_inc(tile_done, 1)
                        continue
                    read(pe, "y3", NB - 1)
                    ops = []
                    for y in (y_high, y_low):
                        ops += [(counts_of(j, i * P, (i + 1) * P), y[:, j, :].bitcast(F32)) for j in range(NB)]
                        ops += [(ident[:], y[:, i, :].bitcast(F32))]
                    for m, (s_, mv) in enumerate(ops):
                        ins = pe.matmul(b, s_, mv, start=(m == 0), stop=(m == len(ops) - 1))
                    ins.then_inc(tile_done, 1)

            def again_tile(name, i):
                n = index[(name, i)]
                read(pe, *tiles[n - WB][:2])
                return work[:, n % WB, :]

            with pe.If(over > 0):
                h3(True)
            with pe.Else():
                h3(False)
            pe.wait_ge(w2_low, 1)
            for i in range(NB):
                y_tile("y3", i, w12_high, w12_low,
                       lambda k: pe.wait_ge(row_low, 2 * KD + KD * (i // HALF) + k + 1) if i % HALF == 0 else None)\
                    .then_inc(tile_done, 1)
            with pe.If(over > 0):
                h4(True)
            with pe.Else():
                h4(False)

        @block.vector
        def _(dve):
            steps = {"prep": 0, "norm": 0}

            def chain(ins):
                steps["prep"] += 1
                ins.then_inc(prep, 1)
                return steps["prep"]

            dve.wait_ge(consts, N_CONSTS)
            chain(dve.tensor_scalar(ident[:], ramp[:, 0:P], pidx, None, ALU.is_equal))
            dve.wait_ge(prep, 1)
            dve.tensor_scalar(neg_ident[:], ident[:], -1.0, None, ALU.mult).then_inc(neg_ready, 1)
            dve.wait_ge(edges_in, 48)
            chain(dve.tensor_copy(dst_f[:], dst_i[:]))
            chain(dve.tensor_scalar(hi_i[:], src_i[:], 7, None, ALU.arith_shift_right))
            chain(dve.tensor_scalar(lo_i[:], src_i[:], P - 1, None, ALU.bitwise_and))
            chain(dve.tensor_copy(w_high[:], w_e[:]))
            dve.wait_ge(prep, 2)
            chain(dve.tensor_reduce(base_max[:, 0:1], dst_f[:], AX.X, ALU.min))
            dve.wait_ge(prep, 4)
            chain(dve.tensor_copy(hi_f[:], hi_i[:]))
            chain(dve.tensor_copy(lo_f[:], lo_i[:]))
            dve.wait_ge(prep, 6)
            chain(dve.tensor_tensor(w_low[:], w_e[:], w_high[:].bitcast(F32), ALU.subtract))
            chain(dve.tensor_scalar(base_max[:, 0:1], base_max[:, 0:1], float(N - WINDOW), None, ALU.min))
            dve.wait_ge(prep, 10)
            chain(dve.tensor_scalar(col_f[:], dst_f[:], base_max[:, 0:1], float(NB),
                                    ALU.subtract, ALU.mult))
            dve.wait_ge(prep, 11)
            chain(dve.tensor_tensor(col_f[:], col_f[:], hi_f[:], ALU.add))
            dve.wait_ge(prep, 12)
            chain(dve.tensor_reduce(base_max[:, 1:2], col_f[:], AX.X, ALU.max))
            assert steps["prep"] == PREP_TURN
            dve.wait_ge(tile_done, 1)
            dve.tensor_copy(tables[:, 0:4, :].rearrange("p a b -> p (a b)"), bank("tab", 0)).then_inc(vector_freed, 1)
            dve.wait_ge(tile_done, 2)
            chain(dve.tensor_copy(tables[:, 4:6, :].rearrange("p a b -> p (a b)"), bank("tab", 1)[:, 0:2 * P]))
            chain(dve.tensor_scalar(base_row[:], bank("tab", 1)[0:1, 2 * P:3 * P], float(NB), None, ALU.mult))
            dve.tensor_reduce(max_col, bank("tab", 1)[0:1, 3 * P:4 * P], AX.X, ALU.max).then_inc(vector_freed, 1)
            dve.wait_ge(vector_freed, 2)
            chain(dve.tensor_scalar(flags[0:1, 0:1], max_col, float(WC), None, ALU.is_ge))
            dve.wait_ge(prep, steps["prep"])

            HG = G // 2

            def make_hot(buf, c, j):
                cols = bass.ds(c + j, HG)
                return dve.tensor_tensor(hot[:, buf, 1, j:j + HG, :],
                                         ramp[:, 0:WC].unsqueeze(1).broadcast_to([P, HG, WC]),
                                         tables[:, 0, cols].unsqueeze(2).broadcast_to([P, HG, WC]), ALU.is_equal)

            def make_sel(buf, c, j):
                cols = bass.ds(c + j, HG)
                return dve.tensor_tensor(sel[:, buf, j:j + HG, :], ramp[:].unsqueeze(1).broadcast_to([P, HG, P]),
                                         tables[:, 1, cols].unsqueeze(2).broadcast_to([P, HG, P]), ALU.is_equal)

            base_regs = [dve.alloc_register(f"base{j}") for j in range(G)]

            def load_bases(c):
                dve.load(base_regs, base_row[0:1, bass.ds(c, G)])
                return [dve.snap(r, min_val=0, max_val=(N - WINDOW) * NB) for r in base_regs]

            def add_window(buf, j, base):
                into = adj[:, :, bass.ds(base, WC)]
                dve.tensor_tensor(into, into, win[:, buf, j, 0:2 * WC].rearrange("p (a b) -> p a b", a=2),
                                  ALU.add).then_inc(added, 1)

            for g in range(2):
                make_hot(g, g * G, 0).then_inc(hot_ready, 1)
                make_hot(g, g * G, HG).then_inc(hot_ready, 1)
                make_sel(g, g * G, 0).then_inc(sel_ready, 1)
                make_sel(g, g * G, HG).then_inc(sel_ready, 1)
            dve.wait_ge(zeros, 3)
            TURN = 2 * BUFS
            turns = (NG - 2) // TURN
            assert turns * TURN == NG - 2
            with dve.Fori(0, turns) as t:
                for q in range(TURN):
                    buf, ahead = (q + 2) % BUFS, (t * TURN + q + 2) * G
                    bases = load_bases((t * TURN + q) * G)
                    dve.wait_ge(group_done, t * TURN + q + 2)
                    makes = [(make_hot, 0, hot_ready), (make_hot, HG, hot_ready),
                             (make_sel, 0, sel_ready), (make_sel, HG, sel_ready)]
                    for j in range(G):
                        if q + j > 0:
                            dve.wait_ge(added, (t * TURN + q) * G + j)
                        add_window(q % 2, j, bases[j])
                        make, half, ready = makes[j]
                        make(buf, ahead, half).then_inc(ready, 1)
                dve.wait_ge(added, t * (TURN * G) + TURN * G)
            for g in (NG - 2, NG - 1):
                bases = load_bases(g * G)
                dve.wait_ge(group_done, g + 2)
                for j in range(G):
                    dve.wait_ge(added, g * G + j)
                    add_window(g % 2, j, bases[j])
            dve.wait_ge(added, CH)

            uncovered = dve.value_load(flags[0:1, 0:1], min_val=0, max_val=1)
            with dve.If(uncovered > 0):
                dve.wait_ge(whigh_ready, NG)
                dve.wait_ge(wlow_ready, NG)
                dve.wait_ge(tile_done, index[("wgt1", KD - 1)] + 1)
                for q in range(BANK // P):
                    dve.tensor_scalar(gen_ramp[:, q * P:(q + 1) * P], ramp[:], float(q * P), None, ALU.add)\
                        .then_inc(gen_added, 1)
                dve.wait_ge(gen_added, BANK // P)
                gm = lambda ins, n: (ins.then_inc(gen_mask, 1), dve.wait_ge(gen_mask, n))
                gm(dve.tensor_scalar(tables[:, 0, :], tables[:, 0, :], float(WC), None, ALU.is_ge), 1)
                gm(dve.tensor_tensor(tables[:, 2, :], tables[:, 2, :], tables[:, 0, :], ALU.mult), 2)
                gm(dve.tensor_tensor(tables[:, 3, :], tables[:, 3, :], tables[:, 0, :], ALU.mult), 3)
                gm(dve.tensor_scalar(tables[:, 5, :], tables[:, 5, :], 1.0, None, ALU.add), 4)
                gm(dve.tensor_tensor(tables[:, 5, :], tables[:, 5, :], tables[:, 0, :], ALU.mult), 5)
                gm(dve.tensor_scalar(tables[:, 5, :], tables[:, 5, :], -1.0, float(P), ALU.add, ALU.mult), 6)
                gm(dve.tensor_tensor(tables[:, 5, :], tables[:, 5, :], tables[:, 1, :], ALU.add), 7)
                with dve.Fori(0, 2) as hf:
                    with dve.Fori(0, NB) as hb:
                        with dve.Fori(0, CH) as c:
                            n = (hf * NB + hb) * CH + c
                            col = bass.ds(c, 1)
                            gen_m = hot_all[:, 0:3 * BANK]
                            dve.tensor_scalar(sel[:, 0, 0, :], ramp[:, 0:P], tables[:, 5, col], None,
                                              ALU.is_equal)
                            dve.tensor_scalar(gen_m[:, 0:BANK], gen_ramp, tables[:, 4, col],
                                              tables[:, 2, col], ALU.is_equal, ALU.mult)
                            dve.tensor_scalar(gen_m[:, BANK:2 * BANK], gen_ramp, tables[:, 4, col],
                                              tables[:, 3, col], ALU.is_equal, ALU.mult)
                            dve.tensor_scalar(gen_m[:, 2 * BANK:3 * BANK], gen_ramp, tables[:, 4, col], None,
                                              ALU.is_equal).then_inc(gen_ready, 1)
                            dve.wait_ge(gen_done, n + 1)
                            for kind in range(2):
                                into = adj[:, kind, bass.ds(hf * BANK * NB + hb, BANK, step=NB)]
                                dve.tensor_tensor(into, into,
                                                  win[:, 0, 2 * kind:2 * kind + 2, :].rearrange("p a b -> p (a b)"),
                                                  ALU.add).then_inc(gen_added, 1)
                            dve.wait_ge(gen_added, BANK // P + 2 * n + 2)
                        dve.tensor_scalar(tables[:, 5, :], tables[:, 5, :], -float(P), None, ALU.add)\
                            .then_inc(gen_mask, 1)
                        dve.wait_ge(gen_mask, 8 + hf * (NB + 2) + hb)
                    dve.tensor_scalar(tables[:, 5, :], tables[:, 5, :], float(N), None, ALU.add)\
                        .then_inc(gen_mask, 1)
                    dve.tensor_scalar(tables[:, 4, :], tables[:, 4, :], -float(BANK), None, ALU.add)\
                        .then_inc(gen_mask, 1)
                    dve.wait_ge(gen_mask, 7 + (hf + 1) * (NB + 2))
            with dve.Else():
                dve.engine_nop()
            dve.sem_inc(adj_ready, 1)

            def step(ins):
                steps["norm"] += 1
                ins.then_inc(norm, 1)
                dve.wait_ge(norm, steps["norm"])
            step(dve.tensor_reduce(deg, adj[:, 0, :].rearrange("p (d h) -> p h d", h=NB), AX.X, ALU.add))
            step(dve.tensor_scalar(deg_pos, deg, 0.0, None, ALU.is_gt))
            dve.tensor_scalar(deg_safe, deg, 1.2e-38, None, ALU.max).then_inc(deg_ready, 1)
            dve.wait_ge(pow_ready, 1)
            dve.tensor_tensor(dinv, dinv, deg_pos, ALU.mult).then_inc(dinv_ready, 1)

            def tile_wait(name, i=0, more=0):
                dve.wait_ge(tile_done, index[(name, i)] + 1 + more)

            highs = [0]

            def lower(name, i, dest, high, scale=1.0, more=0):
                highs[0] += 1
                tile_wait(name, i, more)
                dve.wait_ge(high_ready, highs[0])
                tile = bank(name, i)
                if name == "at":
                    tile = tile.rearrange("p (b n) -> p b n", b=HALF)
                dve.scalar_tensor_tensor(out=dest, in0=shaped(tile, name), scalar=scale, in1=high.bitcast(F32),
                                         op0=ALU.mult, op1=ALU.subtract).then_inc(vector_freed, 1)

            for name, n, _ in mixed:
                if name == "at":
                    j, h = divmod(n, 2)
                    lower("at", n, at_low[:, j, h * BANK:(h + 1) * BANK].rearrange("p (b n) -> p b n", b=HALF),
                          at_high[:, h * HALF:(h + 1) * HALF, j, :], dinv[:, j:j + 1], more=1 - h)
                elif name == "dinvb":
                    tile_wait(name, n)
                    dve.tensor_copy(col_scale[:, n * BANK:(n + 1) * BANK], bank(name, n)).then_inc(vector_freed, 1)

            n_rows = [0]

            def row_scale(name, n):
                n_rows[0] += 1
                r = n_rows[0]
                tile_wait(name, n)
                if r > 3:
                    dve.wait_ge(row_low, r - 3)
                h = n // KD
                dve.tensor_tensor(tmp[:, (r - 1) % 3, :], bank(name, n), col_scale[:, h * BANK:(h + 1) * BANK],
                                  ALU.mult).then_inc(vector_freed, 1)
                return r

            def leak(r):
                row = tmp[:, (r - 1) % 3, :]
                dve.wait_ge(row_biased, r)
                dve.scalar_tensor_tensor(out=row, in0=row, scalar=SLOPE, in1=row, op0=ALU.mult,
                                         op1=ALU.max).then_inc(row_leaked, 1)

            tile_wait("y0", NB - 1)
            dve.wait_ge(split_low, len(split_count))
            read(dve, "dinvb", 1)
            for n in range(2 * KD):
                leak(row_scale("h1", n))
                if n == 1:
                    dve.memset(ones_mat[:], 1.0).then_inc(ones_ready, 1)
                    dve.wait_ge(ones_ready, 1)
                    dve.tensor_reduce(cnt_sums[:], adj[:, 1, :].rearrange("p (d h) -> p d h", h=NB), AX.X,
                                      ALU.add).then_inc(sums_ready, 1)
            tile_wait("deg1")
            dve.tensor_scalar(deg1, bank("deg1")[:, 0:NB], 1.0, None, ALU.add).then_inc(vector_freed, 1)
            for b in range(NB):
                lower("y1", b, y_low[:, b, :], y_high[:, b, :])
            for h in range(2):
                tile_wait("disb", h)
                dve.tensor_copy(col_scale[:, h * BANK:(h + 1) * BANK], bank("disb", h)).then_inc(vector_freed, 1)
            read(dve, "disb", 1)
            step(dve.tensor_reduce(overflow, col_scale[:], AX.X, ALU.min))
            dve.tensor_scalar(flags[0:1, 1:2], overflow[0:1, :], EXACT_DEGREE ** -0.5, None, ALU.is_lt)\
                .then_inc(overflow_ready, 1)

            def layer_norm(b, z, dest, count):
                st, mv = stats[:, 6 * (b % 2):6 * (b % 2) + 6], mean_var[:, 2 * (b % 2):2 * (b % 2) + 2]
                r = rstd[:, 2 * (b % 2):2 * (b % 2) + 2]
                step(dve.bn_stats(st, z))
                step(dve.bn_aggr(mv, st))
                dve.tensor_scalar(r[:, 0:1], mv[:, 1:2], EPS, None, ALU.add).then_inc(var_ready, 1)
                dve.wait_ge(rstd_ready, count)
                return dve.tensor_scalar(dest, z, mv[:, 0:1], r[:, 1:2], ALU.subtract, ALU.mult)

            def scaled(b):
                return tmp[:, b % 3, :]

            def low_of(name, i):
                if name == "x1t":
                    lower(name, i, ht_low[:, :, i * P:(i + 1) * P], ht_high[:, :, i * P:(i + 1) * P])
                else:
                    lower(name, i, y_low[:, i, :], y_high[:, i, :], dis[:, i:i + 1])

            dve.wait_ge(row_low, 2 * KD)
            dve.wait_ge(x_again_in, 16)
            for b in range(NB):
                tile_wait("h2", b)
                z = scaled(b)
                dve.scalar_tensor_tensor(out=z, in0=bank("h2", b), scalar=dinv[:, b:b + 1],
                                         in1=bias_bc[:, 0, :], op0=ALU.mult, op1=ALU.add).then_inc(vector_freed, 1)
                read(dve, "h2", b)
                step(dve.scalar_tensor_tensor(out=z, in0=z, scalar=SLOPE, in1=z, op0=ALU.mult, op1=ALU.max))
                step(dve.tensor_tensor(z, z, xs[:, b, :], ALU.add))
                layer_norm(b, z, xs[:, b, :], b + 1).then_inc(x1_ready, 1)
                if b > 0:
                    low_of("x1t", b - 1)
            for i in range(NB):
                if i == NB - 1:
                    low_of("x1t", i)
                low_of("y2", i)
            for n in range(2 * KD):
                row_scale("h3", n)
            for i in range(NB):
                low_of("y3", i)
            dve.wait_ge(b2_in, 16)
            dve.wait_ge(row_low, 4 * KD)
            for b in range(NB):
                tile_wait("h4", b)
                z = scaled(b)
                dve.scalar_tensor_tensor(out=z, in0=bank("h4", b), scalar=dis[:, b:b + 1],
                                         in1=bias_bc[:, 1, :], op0=ALU.mult, op1=ALU.add).then_inc(vector_freed, 1)
                read(dve, "h4", b)
                step(dve.tensor_tensor(z, z, xs[:, b, :], ALU.add))
                layer_norm(b, z, xs[:, b, :], NB + b + 1).then_inc(out_ready, 1)


INPUTS = ["x", "src", "dst", "edge_weight", "L0_gnn_W_gcn", "L0_gnn_b_gcn", "L0_gnn_W_mlp", "L0_gnn_b_mlp",
          "L1_gnn_W1", "L1_gnn_b1", "L1_gnn_W2", "L1_gnn_b2"]


def kernel(**inputs):
    import numpy as np
    import concourse.bacc as bacc
    from concourse.bass_utils import run_bass_kernel_spmd

    nc = bacc.Bacc("TRN2", target_bir_lowering=False, num_devices=1)
    arrays, args = {}, []
    for name in INPUTS:
        a = np.ascontiguousarray(inputs[name])
        arrays[f"in_{name}"] = a
        args.append(nc.dram_tensor(f"in_{name}", a.shape, mybir.dt.from_np(a.dtype), kind="ExternalInput").ap())
    out = nc.dram_tensor("out", inputs["x"].shape, F32, kind="ExternalOutput").ap()
    gnn_resnorm(nc, *args, out)
    r = run_bass_kernel_spmd(nc, [arrays], core_ids=[0])
    return r.results[0]["out"]
```

```python
from contextlib import ExitStack

import concourse.bass as bass
from concourse import mybir

F32 = mybir.dt.float32
F32R = mybir.dt.float32r
I32 = mybir.dt.int32
ALU = mybir.AluOpType
ACT = mybir.ActivationFunctionType
AX = mybir.AxisListType

P = 128
BANK = 512
WINDOW = 12
BUFS = 3
G = 4
SLOPE = 0.01
EPS = 1e-5
PREP_PARTS, PREP_COLUMNS, PREP_BASES = 9, 12, 13
N_CONSTS = 4
EXACT_DEGREE = 4000.0


def gnn_resnorm(nc, x, src, dst, weight, wg, bg, wm, bm, w1, b1, w2, b2, out):
    N, D = x.shape
    E = src.shape[0]
    NB = N // P
    KD = D // P
    CH = E // P
    NG = CH // G
    WC = WINDOW * NB
    HALF = NB // 2
    assert D == BANK and CH == P and N * 1 == 2 * BANK and NB == 8 and KD == 4

    with ExitStack() as ctx:
        start = (nc.sbuf_base + 31) // 32 * 32
        KB = 1024
        ADJ, ATH, YR, HR, XR, WR, SM = (start + k * KB for k in (0, 64, 96, 128, 160, 176, 192))
        cursor = {}

        def at(name, region, shape, dtype):
            size = 4
            for n in shape[1:]:
                size *= n
            offset = cursor.get(region, region)
            cursor[region] = offset + (size + 31) // 32 * 32
            return nc.alloc_sbuf_tensor_at(name, shape, dtype, offset=offset)

        def again(region):
            cursor[region] = region

        adj = at("adj", ADJ, [P, 2, N * NB], F32)
        again(ADJ)
        at_low = at("at_low", ADJ, [P, NB, N], F32R)
        sel = at("sel", ATH, [P, BUFS, G, P], F32R)
        hot_row = (3 * BUFS * G + 1) * WC
        hot_all = at("hot", ATH, [P, hot_row], F32R)
        hot = hot_all[:, 0:3 * BUFS * G * WC].rearrange("p (b a g c) -> p b a g c", b=BUFS, a=3, g=G)
        ramp = at("ramp", ATH, [P, P], F32)
        tables = at("tables", ATH, [P, 6, P], F32)
        w_raw = at("w_raw", ATH, [P, KD, D], F32)
        gen_ramp = w_raw[:, 0, :]
        assert cursor[ATH] <= YR
        again(ATH)
        at_high = at("at_high", ATH, [P, NB, NB, P], F32R)
        again(ATH)
        cnt = at("cnt", ATH, [P, NB, NB, P], F32R)
        wgta_high = at("wgta_high", YR, [P, KD, D], F32R)
        wgta_low = at("wgta_low", YR, [P, KD, D], F32R)
        wma_high = at("wma_high", YR, [P, KD, D], F32R)
        wm_raw = at("wm_raw", YR, [P, KD, D], F32)
        cursor[YR] -= 4 * KD * D
        wma_low = at("wma_low", YR, [P, KD, D], F32R)
        again(YR)
        y_high = at("y_high", YR, [P, NB, D], F32R)
        y_low = at("y_low", YR, [P, NB, D], F32R)
        ht_high = at("ht_high", HR, [P, KD, N], F32R)
        ht_low = at("ht_low", HR, [P, KD, N], F32R)
        x_first = at("x_first", XR, [P, NB, D], F32)
        again(XR)
        wgtb_high = at("wgtb_high", XR, [P, KD, D], F32R)
        wgtb_low = at("wgtb_low", XR, [P, KD, D], F32R)
        again(XR)
        cnt_sums = at("cnt_sums", XR, [P, N], F32)
        ones_mat = at("ones_mat", XR, [P, 2], F32)
        again(XR)
        xs = at("xs", XR, [P, NB, D], F32)
        wca_high = at("wca_high", WR, [P, KD, D], F32R)
        wca_low = at("wca_low", WR, [P, KD, D], F32R)
        again(WR)
        wcb_high = at("wcb_high", WR, [P, KD, D], F32R)
        wcb_low = at("wcb_low", WR, [P, KD, D], F32R)
        again(WR)
        w12_high = at("w12_high", WR, [P, KD, D], F32R)
        w12_raw = at("w12_raw", WR, [P, KD, D], F32)
        cursor[WR] -= 4 * KD * D
        w12_low = at("w12_low", WR, [P, KD, D], F32R)
        tmp = at("tmp", SM, [P, 3, BANK], F32)
        again(SM)
        cursor[SM] += 2 * 4 * BANK
        bias_rows = at("bias_rows", SM, [3, D], F32)
        col_scale = at("col_scale", SM, [P, N], F32)
        bias_bc = at("bias_bc", SM, [P, 2, D], F32)
        ident = at("ident", SM, [P, P], F32)
        neg_ident = at("neg_ident", SM, [P, P], F32R)
        small = at("small", SM, [P, 104], F32)
        bg_raw = at("bg_raw", SM, [P, KD], F32)
        bg_parts = at("bg_parts", SM, [P, KD, 2], F32R)
        flags = at("flags", SM, [1, 8], I32)
        assert cursor[SM] <= nc.sbuf_usable_end, (cursor[SM], nc.sbuf_usable_end)
        EDGE = start + 192 * KB + 4 * 3 * BANK
        src_i = at("src_i", EDGE, [P, P], I32)
        dst_i = at("dst_i", EDGE, [P, P], I32)
        w_e = at("w_e", EDGE, [P, P], F32)
        dst_f = at("dst_f", EDGE, [P, P], F32)
        hi_i = at("hi_i", EDGE, [P, P], I32)
        lo_i = at("lo_i", EDGE, [P, P], I32)
        hi_f = at("hi_f", EDGE, [P, P], F32)
        lo_f = at("lo_f", EDGE, [P, P], F32)
        col_f = at("col_f", EDGE, [P, P], F32)
        w_high = at("w_high", EDGE, [P, P], F32R)
        w_low = at("w_low", EDGE, [P, P], F32)
        ones3 = at("ones3", EDGE, [3, P], F32)
        base_row = at("base_row", EDGE, [1, P], I32)
        assert cursor[EDGE] <= EDGE + 8 * KB

        deg = small[:, 0:8]
        dinv = small[:, 8:16]
        dis = small[:, 16:24]
        power = small[:, 24:32]
        deg_pos = small[:, 32:40]
        deg_safe = small[:, 40:48]
        base_max = small[:, 48:50]
        pidx = small[:, 50:51]
        bias_t = small[:, 52:56]
        b1_t = small[:, 56:60]
        stats = small[:, 60:72]
        mean_var = small[:, 72:76]
        rstd = small[:, 76:80]
        overflow = small[:, 80:81]
        deg1 = small[:, 84:92]
        max_col = small[0:1, 100:101]

        wgt_parts = ((wgta_high, wgta_low), (wgtb_high, wgtb_low))
        wm_parts = ((wma_high, wma_low), (ht_high[:, :, 0:D], ht_low[:, :, 0:D]))
        wm_raws = (wm_raw, w_raw)

        win = ctx.enter_context(nc.psum_tensor("win", [P, 2, G, 256], F32))
        work = ctx.enter_context(nc.psum_tensor("work", [P, 4, BANK], F32))
        WB = 4

        SCALAR, VECTOR, REST = "scalar", "vector", "rest"
        tiles = [("tab", 0, VECTOR), ("tab", 1, VECTOR)]
        first_fill = len(tiles)
        wgt = [[(f"wgt{l}", k, SCALAR) for k in range(KD)] for l in (0, 1)]
        wc = [[(f"wc{l}", k, REST) for k in range(KD)] for l in (0, 1)]
        xt = [("xt", b, SCALAR) for b in range(NB)]
        y0 = [("y0", b, REST) for b in range(NB)]
        bias, biasb = [[(f"{b}{l}", 0, SCALAR) for l in (0, 1)] for b in ("bias", "biasb")]
        table = {0: [wgt[0][0]], 1: [wgt[0][1]], 2: [wgt[0][2]], 3: [wgt[0][3]],
                 6: [xt[0]], 7: [xt[1]], 8: [xt[2]], 9: [wc[0][0]], 10: [xt[3]], 11: [wc[0][1]], 12: [xt[4]],
                 13: [wc[0][2]], 14: [xt[5]], 15: [wc[0][3]], 16: [xt[6]], 17: [bias[0]], 18: [xt[7]], 19: [y0[0]],
                 20: [wgt[1][0]], 21: [y0[1]], 22: [wgt[1][1]], 23: [y0[2], wgt[1][2]], 24: [wgt[1][3]], 25: [y0[3]],
                 26: [biasb[0]], 27: [y0[4]], 29: [y0[5]], 31: [y0[6]]}
        slots = [table.get(n, []) for n in range(NG)]
        wm_slots = {3 + k: (0, k) for k in range(KD)} | {28 + k: (1, k) for k in range(KD)}
        tiles += [t for slot in slots for t in slot]
        slot = lambda n: slots[n] if 0 <= n < NG else []
        fills = tiles[first_fill:]
        late_rest = [t for t in slots[NG - 2] + slots[NG - 1] if t[2] == REST]
        mixed = [y0[NB - 1], bias[1], wc[1][0], biasb[1]]
        between = {0: wc[1][1], 1: wc[1][2], 3: wc[1][3], 4: ("dinvb", 0, VECTOR), 5: ("dinvb", 1, VECTOR)}
        for j in range(NB):
            mixed += [("at", 2 * j, VECTOR), ("at", 2 * j + 1, VECTOR)]
            mixed += [between[j]] if j in between else []
        tiles += mixed
        tiles += [("h1", f, VECTOR) for f in range(2 * KD)]
        tiles += [("deg1", 0, VECTOR)]
        tiles += [("y1", b, VECTOR) for b in range(NB)]
        tiles += [("disb", h, VECTOR) for h in range(2)]
        tiles += [("h2", 0, VECTOR)]
        for b in range(1, NB):
            tiles += [("h2", b, VECTOR), ("x1t", b - 1, VECTOR)]
        tiles += [("y2", b, VECTOR) for b in range(2)] + [("x1t", NB - 1, VECTOR)]
        tiles += [("y2", b, VECTOR) for b in range(2, NB)]
        tiles += [("h3", f, VECTOR) for f in range(2 * KD)]
        tiles += [("y3", b, VECTOR) for b in range(NB)]
        tiles += [("h4", b, VECTOR) for b in range(NB)]
        index = {t[:2]: n for n, t in enumerate(tiles)}
        done_at, freed = {}, {SCALAR: 0, VECTOR: 0, REST: 0}
        for n, t in enumerate(tiles):
            freed[t[2]] += 1
            done_at[n] = (t[2], freed[t[2]])

        def read(eng, name, i=0):
            who, value = done_at[index[(name, i)]]
            eng.wait_ge({SCALAR: scalar_freed, VECTOR: vector_freed, REST: rest_freed}[who], value)

        def bank(name, i=0):
            return work[:, index[(name, i)] % WB, :]

        sem = lambda name: ctx.enter_context(nc.semaphore(name))
        edges_in = sem("edges_in")
        x_in, x_again_in = sem("x_in"), sem("x_again_in")
        wg_in, wm_in = sem("wg_in"), sem("wm_in")
        bg_in, bm_in = sem("bg_in"), sem("bm_in")
        b1_in, b2_in = sem("b1_in"), sem("b2_in")
        w1_in, w2_in = sem("w1_in"), sem("w2_in")
        consts = sem("consts")
        zeros = sem("zeros")
        prep = sem("prep")
        tile_done = sem("tile_done")
        scalar_freed = sem("scalar_freed")
        neg_ready = sem("neg_ready")
        rest_freed = sem("rest_freed")
        rest_high = sem("rest_high")
        rest_done = sem("rest_done")
        vector_freed = sem("vector_freed")
        sel_ready = sem("sel_ready")
        hot_ready = sem("hot_ready")
        whigh_ready = sem("whigh_ready")
        wlow_ready = sem("wlow_ready")
        group_done = sem("group_done")
        added = sem("added")
        adj_ready = sem("adj_ready")
        gen_ready, gen_done, gen_added = sem("gen_ready"), sem("gen_done"), sem("gen_added")
        gen_mask = sem("gen_mask")
        split_copy = sem("split_copy")
        split_low = sem("split_low")
        wm_split_high, wm_split_low = sem("wm_split_high"), sem("wm_split_low")
        bg_high, bg_split = sem("bg_high"), sem("bg_split")
        deg_ready = sem("deg_ready")
        pow_ready = sem("pow_ready")
        dinv_ready = sem("dinv_ready")
        high_ready = sem("high_ready")
        sums_ready = sem("sums_ready")
        ones_ready = sem("ones_ready")
        row_biased, row_leaked = sem("row_biased"), sem("row_leaked")
        row_high, row_low = sem("row_high"), sem("row_low")
        norm = sem("norm")
        var_ready, rstd_ready = sem("var_ready"), sem("rstd_ready")
        x1_ready = sem("x1_ready")
        res_biased = sem("res_biased")
        cnt_ready = sem("cnt_ready")
        overflow_ready = sem("overflow_ready")
        w1_high, w1_low, w2_high, w2_low = sem("w1_high"), sem("w1_low"), sem("w2_high"), sem("w2_low")
        out_ready, stored = sem("out_ready"), sem("stored")

        split_count, rest_count = {}, {}
        for t in fills + mixed:
            if t[2] == SCALAR and not t[0].startswith("bias"):
                split_count[t[:2]] = len(split_count) + 1
            if t[2] == REST:
                rest_count[t[:2]] = len(rest_count) + 1

        def parts_of(t):
            name, i = t[0], t[1]
            if name.startswith("wgt"):
                return [part[:, i, :] for part in wgt_parts[int(name[-1])]]
            if name == "xt":
                return (ht_high[:, :, i * P:(i + 1) * P], ht_low[:, :, i * P:(i + 1) * P])
            if name == "wc0":
                return wca_high[:, i, :], wca_low[:, i, :]
            if name == "wc1":
                return wcb_high[:, i, :], wcb_low[:, i, :]
            return y_high[:, i, :], y_low[:, i, :]

        def shaped(ap, name):
            return ap.rearrange("p (k n) -> p k n", k=KD) if name in ("xt", "x1t") else ap

        block = ctx.enter_context(nc.Block())

        @block.sync
        def _(sp):
            rows = "(c e) -> c e"
            sp.dma_start(dst_i[:], dst.rearrange(rows, e=P)).then_inc(edges_in, 16)
            sp.dma_start(src_i[:], src.rearrange(rows, e=P)).then_inc(edges_in, 16)
            sp.dma_start(w_e[:], weight.rearrange(rows, e=P)).then_inc(edges_in, 16)
            by_k = "(k p) n -> p k n"
            sp.dma_start(w_raw[:], wg[0].rearrange(by_k, p=P)).then_inc(wg_in, 16)
            sp.dma_start(wm_raw[:], wm[0].rearrange(by_k, p=P)).then_inc(wm_in, 16)
            sp.dma_start(x_first[:], x.rearrange(by_k, p=P)).then_inc(x_in, 16)
            with nc.allow_non_contiguous_dma(reason="bias columns"):
                sp.dma_start(bg_raw[:], bg[0].rearrange("(k p) -> p k", p=P)).then_inc(bg_in, 16)
                sp.dma_start(b1_t, b1.rearrange("(k p) -> p k", p=P)).then_inc(b1_in, 16)
            sp.dma_start(bias_rows[2:3, :], bm[0:1, :]).then_inc(bm_in, 16)
            sp.wait_ge(tile_done, index[("wgt0", KD - 1)] + 1)
            sp.dma_start(w_raw[:], wg[1].rearrange(by_k, p=P)).then_inc(wg_in, 16)
            sp.wait_ge(bg_split, 1)
            with nc.allow_non_contiguous_dma(reason="bias columns"):
                sp.dma_start(bg_raw[:], bg[1].rearrange("(k p) -> p k", p=P)).then_inc(bg_in, 16)
            sp.wait_ge(tile_done, index[("wgt1", KD - 1)] + 1)
            sp.dma_start(w_raw[:], wm[1].rearrange(by_k, p=P)).then_inc(wm_in, 16)
            sp.wait_ge(tile_done, index[("biasb0", 0)] + 1)
            sp.dma_start(bias_rows[2:3, :], bm[1:2, :]).then_inc(bm_in, 16)
            sp.wait_ge(tile_done, index[("biasb1", 0)] + 1)
            sp.wait_ge(adj_ready, 1)
            sp.dma_start(bias_bc[:, 1, :], b2.rearrange("(a n) -> a n", a=1).broadcast_to([P, D])).then_inc(b2_in, 16)
            sp.wait_ge(tile_done, index[("deg1", 0)] + 1)
            sp.dma_start(xs[:], x.rearrange(by_k, p=P)).then_inc(x_again_in, 16)
            sp.wait_ge(tile_done, index[("y1", NB - 1)] + 1)
            sp.dma_start(w12_raw[:], w1.rearrange(by_k, p=P)).then_inc(w1_in, 16)
            sp.wait_ge(tile_done, index[("y2", NB - 1)] + 1)
            sp.dma_start(w12_raw[:], w2.rearrange(by_k, p=P)).then_inc(w2_in, 16)
            for b in range(NB):
                sp.wait_ge(out_ready, b + 1)
                sp.dma_start(out[b * P:(b + 1) * P, :], xs[:, b, :]).then_inc(stored, 16)
            sp.wait_ge(stored, 16 * NB)

        @block.gpsimd
        def _(pool):
            pool.iota(ramp[:], [[1, P]], base=0, channel_multiplier=0,
                      allow_small_or_imprecise_dtypes=True).then_inc(consts, 1)
            pool.iota(pidx, [[0, 1]], base=0, channel_multiplier=1,
                      allow_small_or_imprecise_dtypes=True).then_inc(consts, 1)
            pool.memset(power, -0.5).then_inc(consts, 1)
            pool.memset(ones3[:], 1.0).then_inc(consts, 1)
            pool.memset(hot_all[:, 3 * BUFS * G * WC:].bitcast(F32), 0.0).then_inc(zeros, 1)
            pool.memset(adj[:, 1, :], 0.0).then_inc(zeros, 1)

            def weigh(g):
                pool.wait_ge(hot_ready, 2 * g + 2)
                w = tables[:, 2, g * G:(g + 1) * G].unsqueeze(2).broadcast_to([P, G, WC])
                pool.tensor_tensor(hot[:, g % BUFS, 0], hot[:, g % BUFS, 1].bitcast(F32), w,
                                   ALU.mult).then_inc(whigh_ready, 1)

            def low(t):
                n = split_count[t[:2]]
                read(pool, *t[:2])
                hi, lo = parts_of(t)
                pool.tensor_tensor(lo, shaped(tmp[:, n % 2, :], t[0]), hi.bitcast(F32),
                                   ALU.subtract).then_inc(split_low, 1)

            def to_power(safe, res, count):
                pool.tensor_tensor(res, safe, power[:, 0:count], ALU.pow).then_inc(pow_ready, 1)

            def bg_split_up(l):
                pool.wait_ge(bg_in, 16 * (l + 1))
                if l == 1:
                    pool.wait_ge(tile_done, index[("bias0", 0)] + 1)
                pool.tensor_copy(bg_parts[:, :, 0], bg_raw[:]).then_inc(bg_high, 1)
                pool.wait_ge(bg_high, l + 1)
                pool.tensor_tensor(bg_parts[:, :, 1], bg_raw[:], bg_parts[:, :, 0].bitcast(F32),
                                   ALU.subtract).then_inc(bg_split, 1)

            def wm_lower(l, k):
                pool.wait_ge(wm_split_high, KD * l + k + 1)
                high, low_part = wm_parts[l]
                pool.tensor_tensor(low_part[:, k, :], wm_raws[l][:, k, :], high[:, k, :].bitcast(F32),
                                   ALU.subtract).then_inc(wm_split_low, 1)

            pool.wait_ge(vector_freed, 1)
            weigh(0)
            weigh(1)
            for n in range(NG + 1):
                if n + 2 < NG:
                    weigh(n + 2)
                for t in slot(n - 1):
                    if t[:2] in split_count:
                        low(t)
                if n - 1 in wm_slots:
                    l, k = wm_slots[n - 1]
                    wm_lower(l, k)
                    if k == 0:
                        bg_split_up(l)
            pool.wait_ge(deg_ready, 1)
            to_power(deg_safe, dinv, NB)
            n_rows = [0]

            def row_lower(dest, high):
                n_rows[0] += 1
                n = n_rows[0]
                pool.wait_ge(row_high, n)
                pool.tensor_tensor(dest, tmp[:, (n - 1) % 3, :], high.bitcast(F32),
                                   ALU.subtract).then_inc(row_low, 1)

            def w_lower(ready, high_sem):
                pool.wait_ge(high_sem, 1)
                pool.tensor_tensor(w12_low[:], w12_raw[:], w12_high[:].bitcast(F32),
                                   ALU.subtract).then_inc(ready, 1)

            for n in range(2 * KD):
                h, f = divmod(n, KD)
                row_lower(ht_low[:, f, h * BANK:(h + 1) * BANK], ht_high[:, f, h * BANK:(h + 1) * BANK])
            read(pool, "deg1")
            to_power(deg1, dis, NB)
            for b in range(NB):
                pool.wait_ge(var_ready, b + 1)
                r = rstd[:, 2 * (b % 2):2 * (b % 2) + 2]
                pool.tensor_tensor(r[:, 1:2], r[:, 0:1], power[:, 0:1], ALU.pow).then_inc(rstd_ready, 1)
                pool.wait_ge(tile_done, index[("h2", b)] + 1)
                block_of = adj[:, 1, b * P * NB:(b + 1) * P * NB].rearrange("p (d h) -> p h d", h=NB)
                if b > 0:
                    pool.tensor_copy(cnt[:, b, 0:b, :], block_of[:, 0:b, :]).then_inc(cnt_ready, 1)
                if b < NB - 1:
                    pool.tensor_copy(cnt[:, b, b + 1:NB, :], block_of[:, b + 1:NB, :]).then_inc(cnt_ready, 1)
                pool.tensor_tensor(cnt[:, b, b, :], block_of[:, b, :], ident[:], ALU.add).then_inc(cnt_ready, 1)
            for n in range(2 * KD):
                h, f = divmod(n, KD)
                row_lower(ht_low[:, f, h * BANK:(h + 1) * BANK], ht_high[:, f, h * BANK:(h + 1) * BANK])
                if n == 2:
                    w_lower(w2_low, w2_high)
            for b in range(NB):
                pool.wait_ge(var_ready, NB + b + 1)
                r = rstd[:, 2 * (b % 2):2 * (b % 2) + 2]
                pool.tensor_tensor(r[:, 1:2], r[:, 0:1], power[:, 0:1], ALU.pow).then_inc(rstd_ready, 1)

        @block.scalar
        def _(act):
            def weigh_low(g):
                act.wait_ge(hot_ready, 2 * g + 2)
                for j in range(G):
                    c = g * G + j
                    ins = act.activation(hot[:, g % BUFS, 2, j, :], hot[:, g % BUFS, 1, j, :].bitcast(F32), ACT.Copy,
                                         scale=tables[:, 3, c:c + 1])
                ins.then_inc(wlow_ready, 1)

            def wm_upper(l, k):
                act.wait_ge(wm_in, 16 * (l + 1))
                if l == 1:
                    act.wait_ge(tile_done, index[("y0", KD - 1)] + 1)
                act.activation(wm_parts[l][0][:, k, :], wm_raws[l][:, k, :], ACT.Copy).then_inc(wm_split_high, 1)

            def fill(t):
                name, i = t[0], t[1]
                act.wait_ge(tile_done, index[(name, i)] + 1)
                if name.startswith("bias"):
                    l = int(name[-1])
                    if not name.startswith("biasb"):
                        act.activation(bias_rows[0:2, :], bank(name)[0:2, :], ACT.Copy).then_inc(scalar_freed, 1)
                    elif l == 0:
                        act.activation(bias_t, bank(name)[:, 0:KD], ACT.Copy).then_inc(scalar_freed, 1)
                    else:
                        act.activation(bias_bc[:, 0, :], bank(name), ACT.Copy).then_inc(scalar_freed, 1)
                    return
                hi, lo = parts_of(t)
                if t[:2] in rest_count:
                    if name.startswith("y0") and i == 0:
                        act.wait_ge(wm_split_low, KD)
                    act.activation(hi, bank(name, i), ACT.Copy).then_inc(rest_high, 1)
                    return
                n = split_count[t[:2]]
                if n > 2:
                    act.wait_ge(split_low, n - 2)
                act.activation(tmp[:, n % 2, :], bank(name, i), ACT.Copy).then_inc(split_copy, 1)
                act.activation(hi, shaped(bank(name, i), name), ACT.Copy).then_inc(scalar_freed, 1)

            def rest(t):
                act.wait_ge(rest_done, rest_count[t[:2]])
                act.activation(parts_of(t)[1], bank(*t[:2]), ACT.Copy).then_inc(rest_freed, 1)

            act.wait_ge(consts, N_CONSTS)
            act.activation(adj[:, 0, :].rearrange("p (a b) -> p a b", b=P),
                           ramp[:].unsqueeze(1).broadcast_to([P, N * NB // P, P]), ACT.Copy, scale=0.0)\
                .then_inc(zeros, 1)
            act.wait_ge(vector_freed, 1)
            weigh_low(0)
            weigh_low(1)
            for n in range(NG + 1):
                if n + 2 < NG:
                    weigh_low(n + 2)
                for t in slot(n - 2) if n < NG else []:
                    if t[:2] in rest_count:
                        rest(t)
                for t in slot(n - 1):
                    fill(t)
                if n - 1 in wm_slots:
                    wm_upper(*wm_slots[n - 1])

            def upper(name, i, dest, scale=None):
                act.wait_ge(tile_done, index[(name, i)] + 1)
                kw = {} if scale is None else {"scale": scale}
                tile = bank(name, i)
                if name == "at":
                    tile = tile.rearrange("p (b n) -> p b n", b=HALF)
                act.activation(dest, shaped(tile, name), ACT.Copy, **kw).then_inc(high_ready, 1)

            for t in late_rest:
                rest(t)
            for n, t in enumerate(mixed):
                if t[0] not in ("at", "dinvb"):
                    fill(t)
                if n > 1 and mixed[n - 2][2] == REST:
                    rest(mixed[n - 2])
                if t[0] == "at":
                    j, h = divmod(t[1], 2)
                    if t[1] == 0:
                        act.wait_ge(dinv_ready, 1)
                        act.wait_ge(wm_split_low, 2 * KD)
                    upper("at", t[1], at_high[:, h * HALF:(h + 1) * HALF, j, :], dinv[:, j:j + 1])

            n_rows = [0]

            def row_steps(bias, f, h, leaky):
                n_rows[0] += 1
                n = n_rows[0]
                row = tmp[:, (n - 1) % 3, :]
                read(act, "h1" if leaky else "h3", h * KD + f)
                act.activation(row, row, ACT.Identity if leaky else ACT.Relu, bias=bias[:, f:f + 1])\
                    .then_inc(row_biased, 1)
                if leaky:
                    act.wait_ge(row_leaked, n)
                else:
                    act.wait_ge(row_biased, n)
                act.activation(ht_high[:, f, h * BANK:(h + 1) * BANK], row, ACT.Copy).then_inc(row_high, 1)

            for n in range(2 * KD):
                h, f = divmod(n, KD)
                row_steps(bias_t, f, h, True)
            for b in range(NB):
                upper("y1", b, y_high[:, b, :])
            act.wait_ge(w1_in, 16)
            act.activation(w12_high[:], w12_raw[:], ACT.Copy).then_inc(w1_high, 1)
            for name, i, _ in tiles[index[("x1t", 0)]:index[("y2", NB - 1)] + 1]:
                if name == "x1t":
                    upper(name, i, ht_high[:, :, i * P:(i + 1) * P])
                elif name == "y2":
                    upper(name, i, y_high[:, i, :], dis[:, i:i + 1])
            for n in range(2 * KD):
                h, f = divmod(n, KD)
                row_steps(b1_t, f, h, False)
                if n == 2:
                    act.wait_ge(w2_in, 16)
                    act.activation(w12_high[:], w12_raw[:], ACT.Copy).then_inc(w2_high, 1)
            for b in range(NB):
                upper("y3", b, y_high[:, b, :], dis[:, b:b + 1])

        @block.tensor
        def _(pe):
            state = {"n": 0}

            def begin(name, i=0):
                n = index[(name, i)]
                assert n == state["n"], (name, i, n, state["n"])
                state["n"] += 1
                if n >= WB:
                    read(pe, *tiles[n - WB][:2])
                return work[:, n % WB, :]

            def split_product(dest, stationary, moving, wait=None):
                last = len(stationary) - 1
                for k, ((sh, sl), (mh, ml)) in enumerate(zip(stationary, moving)):
                    if wait is not None:
                        wait(k)
                    pairs = [(sh, mh)]
                    if sl is not None:
                        pairs += [(sl, mh)]
                    if ml is not None:
                        pairs += [(sh, ml)]
                    for n, (s, m) in enumerate(pairs):
                        ins = pe.matmul(dest, s, m, start=(k == 0 and n == 0),
                                        stop=(k == last and n == len(pairs) - 1))
                return ins

            def turn(dest, blocks):
                for n, b in enumerate(blocks):
                    ins = pe.transpose(dest[:, n * P:(n + 1) * P], b, ident[:])
                return ins

            def group(g):
                pe.wait_ge(sel_ready, 2 * g + 2)
                pe.wait_ge(whigh_ready, g + 1)
                pe.wait_ge(wlow_ready, g + 1)
                if g >= 2:
                    pe.wait_ge(added, G * (g - 1) + 1)
                b = g % BUFS
                for j in range(G):
                    into = win[:, g % 2, j, 0:2 * WC]
                    pe.matmul(into, sel[:, b, j, :], hot[:, b, 0:2, j, :], start=True, stop=False)
                    low_at = ((3 * b + 2) * G + j) * WC
                    zero_at = 3 * BUFS * G * WC
                    low_zero = bass.AP(tensor=hot_all, offset=low_at,
                                       ap=[[hot_row, P], [zero_at - low_at, 2], [1, WC]])
                    ins = pe.matmul(into, sel[:, b, j, :], low_zero, start=False, stop=True)
                ins.then_inc(group_done, 1)

            def kblocks(high, low, f=None):
                cut = (lambda a, k: a[:, k, f * P:(f + 1) * P]) if f is not None else (lambda a, k: a[:, k, :])
                return [(cut(high, k), cut(low, k)) for k in range(KD)]

            def halved(t):
                return t[0] in ("wc0", "wc1", "y0", "bias0", "bias1")

            def product(t, half):
                name, i = t[0], t[1]
                if name == "y0":
                    parts = (ht_high, ht_low, wca_high, wca_low)
                    pe.wait_ge(split_low, split_count[("xt", i)])
                    if i == 0:
                        read(pe, "wc0", KD // 2 - 1 if half == 0 else KD - 1)
                else:
                    l = int(name[-1])
                    parts = wgt_parts[l] + wm_parts[l]
                    if i == 0:
                        upto = (half + 1) * KD // 2
                        pe.wait_ge(wm_split_low, KD * l + upto)
                        pe.wait_ge(split_low, split_count[(f"wgt{l}", upto - 1)])
                b = begin(name, i) if half == 0 else bank(name, i)
                if name.startswith("bias"):
                    pe.wait_ge(bg_split, l + 1)
                    for k in range(half * KD // 2, (half + 1) * KD // 2):
                        for n, m in enumerate(wm_parts[l]):
                            ins = pe.matmul(b[0:2, :], bg_parts[:, k, :], m[:, k, :], start=(k == 0 and n == 0),
                                            stop=(k == KD - 1 and n == 1))
                    if half == 1:
                        ins.then_inc(tile_done, 1)
                    return
                s = slice(i * P, (i + 1) * P)
                sh, sl, mh, ml = parts
                for k in range(half * KD // 2, (half + 1) * KD // 2):
                    pe.matmul(b, sh[:, k, s], mh[:, k, :], start=(k == 0), stop=False)
                    pe.matmul(b, sl[:, k, s], mh[:, k, :], start=False, stop=False)
                    ins = pe.matmul(b, sh[:, k, s], ml[:, k, :], start=False, stop=(k == KD - 1))
                if half == 1:
                    ins.then_inc(tile_done, 1)

            def filler(t):
                name, i = t[0], t[1]
                if halved(t):
                    return product(t, 1)
                b = begin(name, i)
                if name.startswith("wgt"):
                    l = int(name[-1])
                    if i == 0:
                        pe.wait_ge(wg_in, 16 * (l + 1))
                    ins = turn(b, [w_raw[:, m, i * P:(i + 1) * P] for m in range(KD)])
                elif name == "xt":
                    if i == 0:
                        pe.wait_ge(x_in, 16)
                    ins = turn(b, [x_first[:, i, k * P:(k + 1) * P] for k in range(KD)])
                elif name.startswith("biasb"):
                    l = int(name[-1])
                    pe.wait_ge(bm_in, 16 * (l + 1))
                    read(pe, f"bias{l}")
                    if l == 0:
                        for f in range(KD):
                            ins = pe.matmul(b[:, f:f + 1], bias_rows[:, f * P:(f + 1) * P], ones3[:, 0:1],
                                            start=True, stop=True)
                    else:
                        ins = pe.matmul(b, ones3[:], bias_rows[:], start=True, stop=True)
                ins.then_inc(tile_done, 1)

            pe.wait_ge(consts, N_CONSTS)
            pe.wait_ge(neg_ready, 1)
            b = begin("tab", 0)
            pe.wait_ge(prep, PREP_PARTS)
            turn(b[:, P:], [lo_f[:], w_high[:].bitcast(F32), w_low[:]]).then_inc(group_done, 1)
            pe.wait_ge(prep, PREP_COLUMNS)
            turn(b, [col_f[:]]).then_inc(tile_done, 1)
            b = begin("tab", 1)
            pe.wait_ge(prep, PREP_BASES)
            turn(b, [dst_f[:], hi_f[:]])
            for n in range(2):
                ins = pe.transpose(b[0:1, (2 + n) * P:(3 + n) * P], base_max[:, n:n + 1], ident[:])
            ins.then_inc(tile_done, 1)

            def subtract_high(t):
                pe.wait_ge(rest_high, rest_count[t[:2]])
                pe.matmul(bank(*t[:2]), neg_ident[:], parts_of(t)[0], start=False, stop=True,
                          skip_group_check=True).then_inc(rest_done, 1)

            for n in range(NG):
                group(n)
                if n == 2:
                    uncovered = pe.value_load(flags[0:1, 0:1], min_val=0, max_val=1)
                for t in slot(n - 2):
                    if t[:2] in rest_count:
                        subtract_high(t)
                for t in slot(n):
                    filler(t)
                for t in slot(n + 1):
                    if halved(t):
                        product(t, 0)
            for t in late_rest:
                subtract_high(t)

            gen_m = hot_all[:, 0:3 * BANK]
            with pe.If(uncovered > 0):
                with pe.Fori(0, 2 * NB) as t:
                    with pe.Fori(0, CH) as c:
                        pe.wait_ge(gen_ready, t * CH + c + 1)
                        first = win[:, 0, 0:2, :].rearrange("p a b -> p (a b)")
                        second = win[:, 0, 2:4, :].rearrange("p a b -> p (a b)")
                        pe.matmul(first, sel[:, 0, 0, :], gen_m[:, 0:BANK], start=True, stop=False)
                        pe.matmul(first, sel[:, 0, 0, :], gen_m[:, BANK:2 * BANK], start=False, stop=True)
                        pe.matmul(second, sel[:, 0, 0, :], gen_m[:, 2 * BANK:3 * BANK], start=True, stop=True)\
                            .then_inc(gen_done, 1)
            with pe.Else():
                pe.nop()

            def y_tile(name, i, high, low, wait=None):
                return split_product(begin(name, i),
                                     [(ht_high[:, k, i * P:(i + 1) * P], ht_low[:, k, i * P:(i + 1) * P])
                                      for k in range(KD)],
                                     kblocks(high, low), wait)

            def spread(name, h, scales):
                b = begin(name, h)
                for n in range(HALF):
                    hb = h * HALF + n
                    ins = pe.matmul(b[:, n * P:(n + 1) * P], scales[:, hb:hb + 1].broadcast_to([P, P]), ident[:],
                                    start=True, stop=True)
                ins.then_inc(tile_done, 1)

            for n, (name, i, _) in enumerate(mixed):
                if halved((name, i)):
                    product((name, i), 0)
                    product((name, i), 1)
                elif name.startswith("bias"):
                    filler((name, i, SCALAR))
                elif name == "at":
                    j, h = divmod(i, 2)
                    if i == 0:
                        pe.wait_ge(adj_ready, 1)
                    turn(begin("at", i), [adj[:, 0, j * P * NB + hb:(j + 1) * P * NB:NB]
                                          for hb in range(h * HALF, (h + 1) * HALF)]).then_inc(tile_done, 1)
                else:
                    if i == 0:
                        pe.wait_ge(dinv_ready, 1)
                    spread("dinvb", i, dinv)
                if n > 1 and mixed[n - 2][2] == REST:
                    subtract_high(mixed[n - 2])

            read(pe, "y0", NB - 1)
            read(pe, "wc1", KD - 1)
            for n in range(2 * KD):
                h, f = divmod(n, KD)
                split_product(begin("h1", n),
                              [(y_high[:, j, f * P:(f + 1) * P], y_low[:, j, f * P:(f + 1) * P])
                               for j in range(NB)],
                              [(at_high[:, h * HALF:(h + 1) * HALF, j, :], at_low[:, j, h * BANK:(h + 1) * BANK])
                               for j in range(NB)],
                              lambda j: read(pe, "at", 2 * j + 1) if n == 0 else None).then_inc(tile_done, 1)
            pe.wait_ge(sums_ready, 1)
            b = begin("deg1")
            for n in range(NB):
                ins = pe.matmul(b[:, n:n + 1], cnt_sums[:, n * P:(n + 1) * P], ones_mat[:, 0:1],
                                start=True, stop=True)
            ins.then_inc(tile_done, 1)
            for i in range(NB):
                y_tile("y1", i, wcb_high, wcb_low,
                       lambda k: pe.wait_ge(row_low, KD * (i // HALF) + k + 1) if i % HALF == 0 else None)\
                    .then_inc(tile_done, 1)
            pe.wait_ge(pow_ready, 2)
            for h in range(2):
                spread("disb", h, dis)
            def x1_turn(i):
                pe.wait_ge(x1_ready, i + 1)
                turn(begin("x1t", i), [xs[:, i, k * P:(k + 1) * P] for k in range(KD)]).then_inc(tile_done, 1)

            for i in range(NB):
                split_product(begin("h2", i),
                              [(at_high[:, i, j, :], at_low[:, j, i * P:(i + 1) * P]) for j in range(NB)],
                              [(y_high[:, j, :], y_low[:, j, :]) for j in range(NB)],
                              lambda j: read(pe, "y1", j) if i == 0 else None).then_inc(tile_done, 1)
                if i > 0:
                    x1_turn(i - 1)
            pe.wait_ge(w1_low, KD)
            pe.wait_ge(overflow_ready, 1)
            over = pe.value_load(flags[0:1, 1:2], min_val=0, max_val=1)
            for i in range(NB):
                if i == 2:
                    x1_turn(NB - 1)
                read(pe, "x1t", i)
                y_tile("y2", i, w12_high, w12_low).then_inc(tile_done, 1)
            pe.wait_ge(cnt_ready, 3 * NB - 2)

            def counts_of(hb, d0, d1):
                return adj[:, 1, d0 * NB + hb:d1 * NB:NB]

            def h3(full):
                for n in range(2 * KD):
                    h, f = divmod(n, KD)
                    b = begin("h3", n) if not full else again_tile("h3", n)
                    s = [(y_high[:, j, f * P:(f + 1) * P], y_low[:, j, f * P:(f + 1) * P]) for j in range(NB)]
                    if not full:
                        split_product(b, s, [(cnt[:, h * HALF:(h + 1) * HALF, j, :], None) for j in range(NB)],
                                      lambda j: read(pe, "y2", j) if n == 0 else None).then_inc(tile_done, 1)
                        continue
                    read(pe, "y2", NB - 1)
                    ops = []
                    for j in range(NB):
                        for y in s[j]:
                            ops.append((b, y.bitcast(F32), counts_of(j, h * BANK, (h + 1) * BANK)))
                            if j // HALF == h:
                                c = (j % HALF) * P
                                ops.append((b[:, c:c + P], y.bitcast(F32), ident[:]))
                    for m, (d, s_, mv) in enumerate(ops):
                        ins = pe.matmul(d, s_, mv, start=(m == 0), stop=(m == len(ops) - 1),
                                        skip_group_check=True)
                    ins.then_inc(tile_done, 1)

            def h4(full):
                for i in range(NB):
                    b = begin("h4", i) if not full else again_tile("h4", i)
                    if not full:
                        split_product(b, [(cnt[:, i, j, :], None) for j in range(NB)],
                                      [(y_high[:, j, :], y_low[:, j, :]) for j in range(NB)],
                                      lambda j: read(pe, "y3", j) if i == 0 else None).then_inc(tile_done, 1)
                        continue
                    read(pe, "y3", NB - 1)
                    ops = []
                    for y in (y_high, y_low):
                        ops += [(counts_of(j, i * P, (i + 1) * P), y[:, j, :].bitcast(F32)) for j in range(NB)]
                        ops += [(ident[:], y[:, i, :].bitcast(F32))]
                    for m, (s_, mv) in enumerate(ops):
                        ins = pe.matmul(b, s_, mv, start=(m == 0), stop=(m == len(ops) - 1))
                    ins.then_inc(tile_done, 1)

            def again_tile(name, i):
                n = index[(name, i)]
                read(pe, *tiles[n - WB][:2])
                return work[:, n % WB, :]

            with pe.If(over > 0):
                h3(True)
            with pe.Else():
                h3(False)
            pe.wait_ge(w2_low, 1)
            for i in range(NB):
                y_tile("y3", i, w12_high, w12_low,
                       lambda k: pe.wait_ge(row_low, 2 * KD + KD * (i // HALF) + k + 1) if i % HALF == 0 else None)\
                    .then_inc(tile_done, 1)
            with pe.If(over > 0):
                h4(True)
            with pe.Else():
                h4(False)

        @block.vector
        def _(dve):
            steps = {"prep": 0, "norm": 0}

            def chain(ins):
                steps["prep"] += 1
                ins.then_inc(prep, 1)
                return steps["prep"]

            HG = G // 2

            def make_hot(buf, c, j):
                cols = bass.ds(c + j, HG)
                return dve.tensor_tensor(hot[:, buf, 1, j:j + HG, :],
                                         ramp[:, 0:WC].unsqueeze(1).broadcast_to([P, HG, WC]),
                                         tables[:, 0, cols].unsqueeze(2).broadcast_to([P, HG, WC]), ALU.is_equal)

            def make_sel(buf, c, j):
                cols = bass.ds(c + j, HG)
                return dve.tensor_tensor(sel[:, buf, j:j + HG, :], ramp[:].unsqueeze(1).broadcast_to([P, HG, P]),
                                         tables[:, 1, cols].unsqueeze(2).broadcast_to([P, HG, P]), ALU.is_equal)

            def make_both(g):
                make_hot(g, g * G, 0).then_inc(hot_ready, 1)
                make_hot(g, g * G, HG).then_inc(hot_ready, 1)
                make_sel(g, g * G, 0).then_inc(sel_ready, 1)
                make_sel(g, g * G, HG).then_inc(sel_ready, 1)

            dve.wait_ge(consts, N_CONSTS)
            chain(dve.tensor_scalar(ident[:], ramp[:, 0:P], pidx, None, ALU.is_equal))
            dve.wait_ge(prep, 1)
            dve.tensor_scalar(neg_ident[:], ident[:], -1.0, None, ALU.mult).then_inc(neg_ready, 1)
            dve.wait_ge(edges_in, 48)
            chain(dve.tensor_copy(dst_f[:], dst_i[:]))
            chain(dve.tensor_scalar(hi_i[:], src_i[:], 7, None, ALU.arith_shift_right))
            chain(dve.tensor_scalar(lo_i[:], src_i[:], P - 1, None, ALU.bitwise_and))
            chain(dve.tensor_copy(w_high[:], w_e[:]))
            dve.wait_ge(prep, 2)
            chain(dve.tensor_reduce(base_max[:, 0:1], dst_f[:], AX.X, ALU.min))
            dve.wait_ge(prep, 4)
            chain(dve.tensor_copy(hi_f[:], hi_i[:]))
            chain(dve.tensor_copy(lo_f[:], lo_i[:]))
            dve.wait_ge(prep, 6)
            chain(dve.tensor_tensor(w_low[:], w_e[:], w_high[:].bitcast(F32), ALU.subtract))
            chain(dve.tensor_scalar(base_max[:, 0:1], base_max[:, 0:1], float(N - WINDOW), None, ALU.min))
            dve.wait_ge(prep, 10)
            chain(dve.tensor_scalar(col_f[:], dst_f[:], base_max[:, 0:1], float(NB),
                                    ALU.subtract, ALU.mult))
            dve.wait_ge(prep, 11)
            chain(dve.tensor_tensor(col_f[:], col_f[:], hi_f[:], ALU.add))
            dve.wait_ge(prep, 12)
            chain(dve.tensor_reduce(base_max[:, 1:2], col_f[:], AX.X, ALU.max))
            assert steps["prep"] == PREP_BASES
            dve.wait_ge(tile_done, 1)
            dve.tensor_copy(tables[:, 0:4, :].rearrange("p a b -> p (a b)"), bank("tab", 0)).then_inc(vector_freed, 1)
            dve.wait_ge(vector_freed, 1)
            make_both(0)
            dve.wait_ge(tile_done, 2)
            chain(dve.tensor_copy(tables[:, 4:6, :].rearrange("p a b -> p (a b)"), bank("tab", 1)[:, 0:2 * P]))
            chain(dve.tensor_scalar(base_row[:], bank("tab", 1)[0:1, 2 * P:3 * P], float(NB), None, ALU.mult))
            dve.tensor_reduce(max_col, bank("tab", 1)[0:1, 3 * P:4 * P], AX.X, ALU.max).then_inc(vector_freed, 1)
            dve.wait_ge(vector_freed, 2)
            chain(dve.tensor_scalar(flags[0:1, 0:1], max_col, float(WC), None, ALU.is_ge))
            dve.wait_ge(prep, steps["prep"])

            TURN = 2 * BUFS
            turns = (NG - 2) // TURN
            assert turns * TURN == NG - 2
            base_regs = [dve.alloc_register(f"base{j}") for j in range(TURN * G)]

            def load_bases(c, groups):
                regs = base_regs[:groups * G]
                dve.load(regs, base_row[0:1, bass.ds(c, groups * G)])
                return [dve.snap(r, min_val=0, max_val=(N - WINDOW) * NB) for r in regs]

            def add_window(buf, j, base):
                into = adj[:, :, bass.ds(base, WC)]
                dve.tensor_tensor(into, into, win[:, buf, j, 0:2 * WC].rearrange("p (a b) -> p a b", a=2),
                                  ALU.add).then_inc(added, 1)

            make_both(1)
            uncovered = dve.value_load(flags[0:1, 0:1], min_val=0, max_val=1)
            dve.wait_ge(zeros, 3)
            dve.sem_inc(added, 1)
            with dve.Fori(0, turns) as t:
                bases = load_bases(t * (TURN * G), TURN)
                for q in range(TURN):
                    buf, ahead = (q + 2) % BUFS, (t * TURN + q + 2) * G
                    makes = [(make_hot, 0, hot_ready), (make_hot, HG, hot_ready),
                             (make_sel, 0, sel_ready), (make_sel, HG, sel_ready)]
                    for j in range(G):
                        if j == 0:
                            dve.wait_ge(group_done, t * TURN + q + 1)
                        make, half, ready = makes[j]
                        make(buf, ahead, half).then_inc(ready, 1)
                        if j == 0:
                            dve.wait_ge(group_done, t * TURN + q + 2)
                        dve.wait_ge(added, (t * TURN + q) * G + j + 1)
                        add_window(q % 2, j, bases[q * G + j])
            bases = load_bases((NG - 2) * G, 2)
            halves = (NG - 2) * G + 1
            for g in (NG - 2, NG - 1):
                dve.wait_ge(group_done, g + 2)
                for j in range(G):
                    for kind in range(2):
                        into = adj[:, kind, bass.ds(bases[(g % 2) * G + j], WC)]
                        dve.wait_ge(added, max(halves - 1, (NG - 2) * G + 1))
                        dve.tensor_tensor(into, into, win[:, g % 2, j, kind * WC:(kind + 1) * WC],
                                          ALU.add).then_inc(added, 1)
                        halves += 1
            dve.wait_ge(added, halves)

            with dve.If(uncovered > 0):
                dve.wait_ge(whigh_ready, NG)
                dve.wait_ge(wlow_ready, NG)
                dve.wait_ge(wm_split_low, 2 * KD)
                for q in range(BANK // P):
                    dve.tensor_scalar(gen_ramp[:, q * P:(q + 1) * P], ramp[:], float(q * P), None, ALU.add)\
                        .then_inc(gen_added, 1)
                dve.wait_ge(gen_added, BANK // P)
                gm = lambda ins, n: (ins.then_inc(gen_mask, 1), dve.wait_ge(gen_mask, n))
                gm(dve.tensor_scalar(tables[:, 0, :], tables[:, 0, :], float(WC), None, ALU.is_ge), 1)
                gm(dve.tensor_tensor(tables[:, 2, :], tables[:, 2, :], tables[:, 0, :], ALU.mult), 2)
                gm(dve.tensor_tensor(tables[:, 3, :], tables[:, 3, :], tables[:, 0, :], ALU.mult), 3)
                gm(dve.tensor_scalar(tables[:, 5, :], tables[:, 5, :], 1.0, None, ALU.add), 4)
                gm(dve.tensor_tensor(tables[:, 5, :], tables[:, 5, :], tables[:, 0, :], ALU.mult), 5)
                gm(dve.tensor_scalar(tables[:, 5, :], tables[:, 5, :], -1.0, float(P), ALU.add, ALU.mult), 6)
                gm(dve.tensor_tensor(tables[:, 5, :], tables[:, 5, :], tables[:, 1, :], ALU.add), 7)
                with dve.Fori(0, 2) as hf:
                    with dve.Fori(0, NB) as hb:
                        with dve.Fori(0, CH) as c:
                            n = (hf * NB + hb) * CH + c
                            col = bass.ds(c, 1)
                            gen_m = hot_all[:, 0:3 * BANK]
                            dve.tensor_scalar(sel[:, 0, 0, :], ramp[:, 0:P], tables[:, 5, col], None,
                                              ALU.is_equal)
                            dve.tensor_scalar(gen_m[:, 0:BANK], gen_ramp, tables[:, 4, col],
                                              tables[:, 2, col], ALU.is_equal, ALU.mult)
                            dve.tensor_scalar(gen_m[:, BANK:2 * BANK], gen_ramp, tables[:, 4, col],
                                              tables[:, 3, col], ALU.is_equal, ALU.mult)
                            dve.tensor_scalar(gen_m[:, 2 * BANK:3 * BANK], gen_ramp, tables[:, 4, col], None,
                                              ALU.is_equal).then_inc(gen_ready, 1)
                            dve.wait_ge(gen_done, n + 1)
                            for kind in range(2):
                                into = adj[:, kind, bass.ds(hf * BANK * NB + hb, BANK, step=NB)]
                                dve.tensor_tensor(into, into,
                                                  win[:, 0, 2 * kind:2 * kind + 2, :].rearrange("p a b -> p (a b)"),
                                                  ALU.add).then_inc(gen_added, 1)
                            dve.wait_ge(gen_added, BANK // P + 2 * n + 2)
                        dve.tensor_scalar(tables[:, 5, :], tables[:, 5, :], -float(P), None, ALU.add)\
                            .then_inc(gen_mask, 1)
                        dve.wait_ge(gen_mask, 8 + hf * (NB + 2) + hb)
                    dve.tensor_scalar(tables[:, 5, :], tables[:, 5, :], float(N), None, ALU.add)\
                        .then_inc(gen_mask, 1)
                    dve.tensor_scalar(tables[:, 4, :], tables[:, 4, :], -float(BANK), None, ALU.add)\
                        .then_inc(gen_mask, 1)
                    dve.wait_ge(gen_mask, 7 + (hf + 1) * (NB + 2))
            with dve.Else():
                dve.engine_nop()
            dve.sem_inc(adj_ready, 1)

            def step(ins):
                steps["norm"] += 1
                ins.then_inc(norm, 1)
                dve.wait_ge(norm, steps["norm"])
            step(dve.tensor_reduce(deg, adj[:, 0, :].rearrange("p (d h) -> p h d", h=NB), AX.X, ALU.add))
            step(dve.tensor_scalar(deg_pos, deg, 0.0, None, ALU.is_gt))
            dve.tensor_scalar(deg_safe, deg, 1.2e-38, None, ALU.max).then_inc(deg_ready, 1)
            dve.wait_ge(pow_ready, 1)
            dve.tensor_tensor(dinv, dinv, deg_pos, ALU.mult).then_inc(dinv_ready, 1)

            def tile_wait(name, i=0, more=0):
                dve.wait_ge(tile_done, index[(name, i)] + 1 + more)

            highs = [0]

            def lower(name, i, dest, high, scale=1.0, more=0):
                highs[0] += 1
                tile_wait(name, i, more)
                dve.wait_ge(high_ready, highs[0])
                tile = bank(name, i)
                if name == "at":
                    tile = tile.rearrange("p (b n) -> p b n", b=HALF)
                dve.scalar_tensor_tensor(out=dest, in0=shaped(tile, name), scalar=scale, in1=high.bitcast(F32),
                                         op0=ALU.mult, op1=ALU.subtract).then_inc(vector_freed, 1)

            for name, n, _ in mixed:
                if name == "at":
                    j, h = divmod(n, 2)
                    lower("at", n, at_low[:, j, h * BANK:(h + 1) * BANK].rearrange("p (b n) -> p b n", b=HALF),
                          at_high[:, h * HALF:(h + 1) * HALF, j, :], dinv[:, j:j + 1], more=1 - h)
                elif name == "dinvb":
                    tile_wait(name, n)
                    dve.tensor_copy(col_scale[:, n * BANK:(n + 1) * BANK], bank(name, n)).then_inc(vector_freed, 1)

            n_rows = [0]

            def row_scale(name, n):
                n_rows[0] += 1
                r = n_rows[0]
                tile_wait(name, n)
                if r > 3:
                    dve.wait_ge(row_low, r - 3)
                h = n // KD
                dve.tensor_tensor(tmp[:, (r - 1) % 3, :], bank(name, n), col_scale[:, h * BANK:(h + 1) * BANK],
                                  ALU.mult).then_inc(vector_freed, 1)
                return r

            def leak(r):
                row = tmp[:, (r - 1) % 3, :]
                dve.wait_ge(row_biased, r)
                dve.scalar_tensor_tensor(out=row, in0=row, scalar=SLOPE, in1=row, op0=ALU.mult,
                                         op1=ALU.max).then_inc(row_leaked, 1)

            tile_wait("wc1", KD - 1)
            dve.wait_ge(split_low, len(split_count))
            read(dve, "dinvb", 1)
            for n in range(2 * KD):
                leak(row_scale("h1", n))
                if n == 1:
                    dve.memset(ones_mat[:], 1.0).then_inc(ones_ready, 1)
                    dve.wait_ge(ones_ready, 1)
                    dve.tensor_reduce(cnt_sums[:], adj[:, 1, :].rearrange("p (d h) -> p d h", h=NB), AX.X,
                                      ALU.add).then_inc(sums_ready, 1)
            tile_wait("deg1")
            dve.tensor_scalar(deg1, bank("deg1")[:, 0:NB], 1.0, None, ALU.add).then_inc(vector_freed, 1)
            for b in range(NB):
                lower("y1", b, y_low[:, b, :], y_high[:, b, :])
            for h in range(2):
                tile_wait("disb", h)
                dve.tensor_copy(col_scale[:, h * BANK:(h + 1) * BANK], bank("disb", h)).then_inc(vector_freed, 1)
            read(dve, "disb", 1)
            step(dve.tensor_reduce(overflow, col_scale[:], AX.X, ALU.min))
            dve.tensor_scalar(flags[0:1, 1:2], overflow[0:1, :], EXACT_DEGREE ** -0.5, None, ALU.is_lt)\
                .then_inc(overflow_ready, 1)

            def layer_norm(b, z, dest, count):
                st, mv = stats[:, 6 * (b % 2):6 * (b % 2) + 6], mean_var[:, 2 * (b % 2):2 * (b % 2) + 2]
                r = rstd[:, 2 * (b % 2):2 * (b % 2) + 2]
                step(dve.bn_stats(st, z))
                step(dve.bn_aggr(mv, st))
                dve.tensor_scalar(r[:, 0:1], mv[:, 1:2], EPS, None, ALU.add).then_inc(var_ready, 1)
                dve.wait_ge(rstd_ready, count)
                return dve.tensor_scalar(dest, z, mv[:, 0:1], r[:, 1:2], ALU.subtract, ALU.mult)

            def scaled(b):
                return tmp[:, b % 3, :]

            def low_of(name, i):
                if name == "x1t":
                    lower(name, i, ht_low[:, :, i * P:(i + 1) * P], ht_high[:, :, i * P:(i + 1) * P])
                else:
                    lower(name, i, y_low[:, i, :], y_high[:, i, :], dis[:, i:i + 1])

            dve.wait_ge(row_low, 2 * KD)
            dve.wait_ge(x_again_in, 16)
            for b in range(NB):
                tile_wait("h2", b)
                z = scaled(b)
                dve.scalar_tensor_tensor(out=z, in0=bank("h2", b), scalar=dinv[:, b:b + 1],
                                         in1=bias_bc[:, 0, :], op0=ALU.mult, op1=ALU.add).then_inc(vector_freed, 1)
                read(dve, "h2", b)
                step(dve.scalar_tensor_tensor(out=z, in0=z, scalar=SLOPE, in1=z, op0=ALU.mult, op1=ALU.max))
                step(dve.tensor_tensor(z, z, xs[:, b, :], ALU.add))
                layer_norm(b, z, xs[:, b, :], b + 1).then_inc(x1_ready, 1)
                if b > 0:
                    low_of("x1t", b - 1)
                if 1 <= b <= KD:
                    dve.wait_ge(w1_high, 1)
                    dve.tensor_tensor(w12_low[:, b - 1, :], w12_raw[:, b - 1, :], w12_high[:, b - 1, :].bitcast(F32),
                                      ALU.subtract).then_inc(w1_low, 1)
            for i in range(NB):
                if i == 2:
                    low_of("x1t", NB - 1)
                low_of("y2", i)
            for n in range(2 * KD):
                row_scale("h3", n)
            dve.wait_ge(b2_in, 16)
            for i in range(NB):
                low_of("y3", i)
                dve.tensor_tensor(xs[:, i, :], xs[:, i, :], bias_bc[:, 1, :], ALU.add).then_inc(res_biased, 1)
            dve.wait_ge(row_low, 4 * KD)
            for b in range(NB):
                tile_wait("h4", b)
                z = scaled(b)
                dve.wait_ge(res_biased, b + 1)
                dve.scalar_tensor_tensor(out=z, in0=bank("h4", b), scalar=dis[:, b:b + 1],
                                         in1=xs[:, b, :], op0=ALU.mult, op1=ALU.add).then_inc(vector_freed, 1)
                read(dve, "h4", b)
                layer_norm(b, z, xs[:, b, :], NB + b + 1).then_inc(out_ready, 1)


INPUTS = ["x", "src", "dst", "edge_weight", "L0_gnn_W_gcn", "L0_gnn_b_gcn", "L0_gnn_W_mlp", "L0_gnn_b_mlp",
          "L1_gnn_W1", "L1_gnn_b1", "L1_gnn_W2", "L1_gnn_b2"]


def kernel(**inputs):
    import numpy as np
    import concourse.bacc as bacc
    from concourse.bass_utils import run_bass_kernel_spmd

    nc = bacc.Bacc("TRN2", target_bir_lowering=False, num_devices=1)
    arrays, args = {}, []
    for name in INPUTS:
        a = np.ascontiguousarray(inputs[name])
        arrays[f"in_{name}"] = a
        args.append(nc.dram_tensor(f"in_{name}", a.shape, mybir.dt.from_np(a.dtype), kind="ExternalInput").ap())
    out = nc.dram_tensor("out", inputs["x"].shape, F32, kind="ExternalOutput").ap()
    gnn_resnorm(nc, *args, out)
    r = run_bass_kernel_spmd(nc, [arrays], core_ids=[0])
    return r.results[0]["out"]
```
